# Optimizing a Trainium2 kernel written in Bass

```python
import numpy as np
import jax
import jax.numpy as jnp

def _softmax(x, axis=-1):
    return jax.nn.softmax(x, axis=axis)

def _gelu(x):
    return jax.nn.gelu(x, approximate=True)

def _silu(x):
    return jax.nn.silu(x)

def _sigmoid(x):
    return jax.nn.sigmoid(x)

def _layernorm(x, axis=-1, eps=1e-05):
    m = jnp.mean(x, axis=axis, keepdims=True)
    v = jnp.var(x, axis=axis, keepdims=True)
    return (x - m) / jnp.sqrt(v + eps)

def _scatter_add(tgt, idx, src, axis=0):
    return tgt.at[idx].add(src)

def _segment_sum(src, seg, n):
    return jax.ops.segment_sum(src, seg, n)
kernel_name = 'mk_macaron_d1_jaxref_r8_3f3598'

def setup_inputs(seed: int=0):
    np.random.seed(seed)
    _w = jnp.asarray

    def _L0_attn_setup():
        import jax, jax.numpy as jnp
        import numpy as np
        B, N, DIM, H = (4, 512, 128, 16)
        HD = DIM // H
        SCALE = HD ** (-0.5)

        def _heads(t, bsz, ntok):
            return t.reshape(bsz, ntok, H, HD).transpose(0, 2, 1, 3)

        def _fwd(x, q_w1, q_b1, q_w2, q_b2, k_w1, k_b1, k_w2, k_b2, v_w, v_b, g_w, g_b, p_w, p_b):
            bsz, ntok, dim = x.shape
            gelu = lambda t: jax.nn.gelu(t, approximate=False)
            q = _heads(jax.nn.softplus(gelu(x @ q_w1.T + q_b1) @ q_w2.T + q_b2), bsz, ntok)
            k = _heads(jax.nn.softplus(gelu(x @ k_w1.T + k_b1) @ k_w2.T + k_b2), bsz, ntok)
            v = _heads(gelu(x @ v_w.T + v_b), bsz, ntok)
            g = _heads(gelu(x @ g_w.T + g_b), bsz, ntok)
            z = jnp.einsum('bhcn,bhc->bhn', q, k.sum(axis=-1)) * SCALE
            z = 1.0 / (z + dim)
            A = jnp.einsum('bhcn,bhcm->bhnm', q, k)
            out = jnp.einsum('bhnm,bhdm->bhdn', A, v) * SCALE
            out = (out + v) * z[:, :, None, :]
            out = out.reshape(bsz, ntok, dim)
            out = out * g.reshape(bsz, ntok, dim)
            return out @ p_w.T + p_b
        key = jax.random.key(seed)
        ks = jax.random.split(key, 16)
        w = lambda k: jax.random.normal(k, (DIM, DIM), jnp.float32) * 0.02
        b = lambda k: jax.random.normal(k, (DIM,), jnp.float32) * 0.02
        return {'x': jax.random.normal(ks[0], (B, N, DIM), jnp.float32), 'q_w1': w(ks[1]), 'q_b1': b(ks[2]), 'q_w2': w(ks[3]), 'q_b2': b(ks[4]), 'k_w1': w(ks[5]), 'k_b1': b(ks[6]), 'k_w2': w(ks[7]), 'k_b2': b(ks[8]), 'v_w': w(ks[9]), 'v_b': b(ks[10]), 'g_w': w(ks[11]), 'g_b': b(ks[12]), 'p_w': w(ks[13]), 'p_b': b(ks[14])}
    _L0_attn_in = _L0_attn_setup()

    def _L0_ffn_setup():
        import jax, jax.numpy as jnp
        import numpy as np
        B, S, DIM = (4, 512, 128)
        BASE_COUPLING = 0.1
        NUM_CYCLES = 3

        def _gelu(x):
            return jax.nn.gelu(x, approximate=False)

        def _coupling_net(h, w1, b1, w2, b2, w3, b3, w4, b4):
            h = _gelu(h @ w1 + b1)
            h = _gelu(h @ w2 + b2)
            h = _gelu(h @ w3 + b3)
            return jax.nn.sigmoid(h @ w4 + b4)

        def _global_net(h, w1, b1, w2, b2, w3, b3):
            h = _gelu(h @ w1 + b1)
            h = _gelu(h @ w2 + b2)
            return jax.nn.sigmoid(h @ w3 + b3)

        def _twist(x):
            o_r, o_i, p_r, p_i = jnp.split(x, 4, axis=-1)
            return jnp.concatenate([p_r, -p_i, -o_r, o_i], axis=-1)
        key = jax.random.key(seed)
        ks = jax.random.split(key, 9)
        d = DIM

        def w(k, fan_in, fan_out):
            return jax.random.normal(k, (fan_in, fan_out), dtype=jnp.float32) / np.sqrt(fan_in).astype(np.float32)
        inp = {'x': jax.random.normal(ks[0], (B, S, d), dtype=jnp.float32)}
        cn_dims = [(d, d), (d, d // 2), (d // 2, d // 4), (d // 4, 1)]
        for i, (a, b) in enumerate(cn_dims):
            inp[f'cn_w{i + 1}'] = w(ks[1 + i], a, b)
            inp[f'cn_b{i + 1}'] = jnp.zeros((b,), dtype=jnp.float32)
        gc_dims = [(d, d // 2), (d // 2, d // 4), (d // 4, 1)]
        for i, (a, b) in enumerate(gc_dims):
            inp[f'gc_w{i + 1}'] = w(ks[5 + i], a, b)
            inp[f'gc_b{i + 1}'] = jnp.zeros((b,), dtype=jnp.float32)
        inp['adaptive_range'] = jnp.full((1,), 0.2, dtype=jnp.float32)
        return inp
    _L0_ffn_in = _L0_ffn_setup()
    _d = {'L0_attn_x': _L0_attn_in['x'], 'L0_attn_q_w1': _L0_attn_in['q_w1'], 'L0_attn_q_b1': _L0_attn_in['q_b1'], 'L0_attn_q_w2': _L0_attn_in['q_w2'], 'L0_attn_q_b2': _L0_attn_in['q_b2'], 'L0_attn_k_w1': _L0_attn_in['k_w1'], 'L0_attn_k_b1': _L0_attn_in['k_b1'], 'L0_attn_k_w2': _L0_attn_in['k_w2'], 'L0_attn_k_b2': _L0_attn_in['k_b2'], 'L0_attn_v_w': _L0_attn_in['v_w'], 'L0_attn_v_b': _L0_attn_in['v_b'], 'L0_attn_g_w': _L0_attn_in['g_w'], 'L0_attn_g_b': _L0_attn_in['g_b'], 'L0_attn_p_w': _L0_attn_in['p_w'], 'L0_attn_p_b': _L0_attn_in['p_b'], 'L0_ffn_cn_w1': _L0_ffn_in['cn_w1'], 'L0_ffn_cn_b1': _L0_ffn_in['cn_b1'], 'L0_ffn_cn_w2': _L0_ffn_in['cn_w2'], 'L0_ffn_cn_b2': _L0_ffn_in['cn_b2'], 'L0_ffn_cn_w3': _L0_ffn_in['cn_w3'], 'L0_ffn_cn_b3': _L0_ffn_in['cn_b3'], 'L0_ffn_cn_w4': _L0_ffn_in['cn_w4'], 'L0_ffn_cn_b4': _L0_ffn_in['cn_b4'], 'L0_ffn_gc_w1': _L0_ffn_in['gc_w1'], 'L0_ffn_gc_b1': _L0_ffn_in['gc_b1'], 'L0_ffn_gc_w2': _L0_ffn_in['gc_w2'], 'L0_ffn_gc_b2': _L0_ffn_in['gc_b2'], 'L0_ffn_gc_w3': _L0_ffn_in['gc_w3'], 'L0_ffn_gc_b3': _L0_ffn_in['gc_b3'], 'L0_ffn_adaptive_range': _L0_ffn_in['adaptive_range']}
    _x0 = _d['L0_attn_x']
    _d['L0_attn_x'] = jax.random.normal(jax.random.fold_in(jax.random.key(seed), 1), (2, 1024, 128), dtype=_x0.dtype)
    del _x0
    return _d

def reference(L0_attn_x, L0_attn_q_w1, L0_attn_q_b1, L0_attn_q_w2, L0_attn_q_b2, L0_attn_k_w1, L0_attn_k_b1, L0_attn_k_w2, L0_attn_k_b2, L0_attn_v_w, L0_attn_v_b, L0_attn_g_w, L0_attn_g_b, L0_attn_p_w, L0_attn_p_b, L0_ffn_cn_w1, L0_ffn_cn_b1, L0_ffn_cn_w2, L0_ffn_cn_b2, L0_ffn_cn_w3, L0_ffn_cn_b3, L0_ffn_cn_w4, L0_ffn_cn_b4, L0_ffn_gc_w1, L0_ffn_gc_b1, L0_ffn_gc_w2, L0_ffn_gc_b2, L0_ffn_gc_w3, L0_ffn_gc_b3, L0_ffn_adaptive_range):

    def _L0_attn_ref(x, q_w1, q_b1, q_w2, q_b2, k_w1, k_b1, k_w2, k_b2, v_w, v_b, g_w, g_b, p_w, p_b):
        import jax, jax.numpy as jnp
        import numpy as np
        B, N, DIM, H = (4, 512, 128, 16)
        HD = DIM // H
        SCALE = HD ** (-0.5)

        def _heads(t, bsz, ntok):
            return t.reshape(bsz, ntok, H, HD).transpose(0, 2, 1, 3)

        def _fwd(x, q_w1, q_b1, q_w2, q_b2, k_w1, k_b1, k_w2, k_b2, v_w, v_b, g_w, g_b, p_w, p_b):
            bsz, ntok, dim = x.shape
            gelu = lambda t: jax.nn.gelu(t, approximate=False)
            q = _heads(jax.nn.softplus(gelu(x @ q_w1.T + q_b1) @ q_w2.T + q_b2), bsz, ntok)
            k = _heads(jax.nn.softplus(gelu(x @ k_w1.T + k_b1) @ k_w2.T + k_b2), bsz, ntok)
            v = _heads(gelu(x @ v_w.T + v_b), bsz, ntok)
            g = _heads(gelu(x @ g_w.T + g_b), bsz, ntok)
            z = jnp.einsum('bhcn,bhc->bhn', q, k.sum(axis=-1)) * SCALE
            z = 1.0 / (z + dim)
            A = jnp.einsum('bhcn,bhcm->bhnm', q, k)
            out = jnp.einsum('bhnm,bhdm->bhdn', A, v) * SCALE
            out = (out + v) * z[:, :, None, :]
            out = out.reshape(bsz, ntok, dim)
            out = out * g.reshape(bsz, ntok, dim)
            return out @ p_w.T + p_b
        return _fwd(x, q_w1, q_b1, q_w2, q_b2, k_w1, k_b1, k_w2, k_b2, v_w, v_b, g_w, g_b, p_w, p_b)

    def _L0_ffn_ref(x, cn_w1, cn_b1, cn_w2, cn_b2, cn_w3, cn_b3, cn_w4, cn_b4, gc_w1, gc_b1, gc_w2, gc_b2, gc_w3, gc_b3, adaptive_range):
        import jax, jax.numpy as jnp
        import numpy as np
        B, S, DIM = (4, 512, 128)
        BASE_COUPLING = 0.1
        NUM_CYCLES = 3

        def _gelu(x):
            return jax.nn.gelu(x, approximate=False)

        def _coupling_net(h, w1, b1, w2, b2, w3, b3, w4, b4):
            h = _gelu(h @ w1 + b1)
            h = _gelu(h @ w2 + b2)
            h = _gelu(h @ w3 + b3)
            return jax.nn.sigmoid(h @ w4 + b4)

        def _global_net(h, w1, b1, w2, b2, w3, b3):
            h = _gelu(h @ w1 + b1)
            h = _gelu(h @ w2 + b2)
            return jax.nn.sigmoid(h @ w3 + b3)

        def _twist(x):
            o_r, o_i, p_r, p_i = jnp.split(x, 4, axis=-1)
            return jnp.concatenate([p_r, -p_i, -o_r, o_i], axis=-1)
        global_context = x.mean(axis=1, keepdims=True)
        gf = _global_net(global_context, gc_w1, gc_b1, gc_w2, gc_b2, gc_w3, gc_b3)
        out = x
        for _ in range(NUM_CYCLES):
            tf = _coupling_net(out, cn_w1, cn_b1, cn_w2, cn_b2, cn_w3, cn_b3, cn_w4, cn_b4)
            combined = 0.7 * gf + 0.3 * tf
            coupling = BASE_COUPLING + adaptive_range * (combined - 0.5) * 2.0
            out = out + coupling * _twist(out)
        return out
    x = L0_attn_x
    x = x + 0.5 * _L0_ffn_ref(_layernorm(x, axis=-1), L0_ffn_cn_w1, L0_ffn_cn_b1, L0_ffn_cn_w2, L0_ffn_cn_b2, L0_ffn_cn_w3, L0_ffn_cn_b3, L0_ffn_cn_w4, L0_ffn_cn_b4, L0_ffn_gc_w1, L0_ffn_gc_b1, L0_ffn_gc_w2, L0_ffn_gc_b2, L0_ffn_gc_w3, L0_ffn_gc_b3, L0_ffn_adaptive_range)
    x = x + _L0_attn_ref(_layernorm(x, axis=-1), L0_attn_q_w1, L0_attn_q_b1, L0_attn_q_w2, L0_attn_q_b2, L0_attn_k_w1, L0_attn_k_b1, L0_attn_k_w2, L0_attn_k_b2, L0_attn_v_w, L0_attn_v_b, L0_attn_g_w, L0_attn_g_b, L0_attn_p_w, L0_attn_p_b)
    x = x + 0.5 * _L0_ffn_ref(_layernorm(x, axis=-1), L0_ffn_cn_w1, L0_ffn_cn_b1, L0_ffn_cn_w2, L0_ffn_cn_b2, L0_ffn_cn_w3, L0_ffn_cn_b3, L0_ffn_cn_w4, L0_ffn_cn_b4, L0_ffn_gc_w1, L0_ffn_gc_b1, L0_ffn_gc_w2, L0_ffn_gc_b2, L0_ffn_gc_w3, L0_ffn_gc_b3, L0_ffn_adaptive_range)
    return x

_drawn_inputs = setup_inputs


def setup_inputs(seed=0):
    import zlib

    import numpy as np

    out = dict(_drawn_inputs(seed))
    spreads = {'L0_ffn_cn_b1': (0.0, 2.0),
     'L0_ffn_cn_b2': (0.0, 2.0),
     'L0_ffn_cn_b3': (0.0, 2.0),
     'L0_ffn_gc_b1': (0.0, 2.0),
     'L0_ffn_gc_b2': (0.0, 2.0)}
    factors = {'L0_attn_q_w1': 8.0,
     'L0_attn_q_b1': 64.0,
     'L0_attn_q_w2': 8.0,
     'L0_attn_q_b2': 64.0,
     'L0_attn_k_w1': 8.0,
     'L0_attn_k_b1': 8.0,
     'L0_attn_k_w2': 8.0,
     'L0_attn_k_b2': 8.0,
     'L0_attn_v_w': 8.0,
     'L0_attn_v_b': 8.0,
     'L0_attn_g_w': 8.0,
     'L0_attn_g_b': 8.0,
     'L0_attn_p_w': 8.0,
     'L0_attn_p_b': 4.247,
     'L0_ffn_cn_w1': 7.007,
     'L0_ffn_cn_w2': 6.439,
     'L0_ffn_cn_w3': 5.581,
     'L0_ffn_cn_w4': 3.595,
     'L0_ffn_gc_w1': 64.0,
     'L0_ffn_gc_w2': 34.993,
     'L0_ffn_gc_w3': 64.0}
    for name, (base, spread) in spreads.items():
        noise = np.random.default_rng([zlib.crc32(name.encode()), seed]).standard_normal(out[name].shape)
        drawn = base * np.exp(spread * noise) if base else spread * noise
        out[name] = jnp.asarray(drawn.astype(out[name].dtype))
    for name, factor in factors.items():
        out[name] = (out[name] * factor).astype(out[name].dtype)
    return out
```

```python
import concourse.bass as bass
import concourse.mybir as mybir
from concourse.alu_op_type import AluOpType as ALU
from contextlib import ExitStack

B, N, D, H = 2, 1024, 128, 16
HD = D // H
SLOTS = B * N // D
T = N // SLOTS
GROUPS, GS = 4, SLOTS // 4
GW = GS * D
CYCLES = 3
ITEMS = CYCLES * GROUPS
SCALE = HD ** -0.5
EPS = 1e-5
EXP_TOP = 2.0 ** 60
BASE_COUPLING = 0.1

EARLY = dict(ident=(0, 128), w1=(128, 256), w1t=(256, 384), vec=(384, 400), sel=(400, 402))
NET = dict(w2=(0, 64), w3=(64, 128), w4=(128, 132), gc1=(132, 196), gc2=(196, 228), gc3=(228, 229))
ATT = dict(q1=(0, 128), k1=(128, 256), v=(256, 384), g=(384, 512), q2=(512, 640), k2=(640, 768),
           p=(768, 896), mask=(896, 1024), ones=(1024, 1152))
VEC = dict(b1=0, b2=1, b3=2, q1=3, k1=4, v=5, b4=6, gc1=7, gc2=8, gc3=9, range=10)
ROWS = dict(g=0, q2=1, k2=2, p=3)


def width(table):
    return max(end for _, end in table.values())


def build(nc, x, early, net, att, rows, out):
    f32, bf16 = mybir.dt.float32, mybir.dt.bfloat16
    ACT = mybir.ActivationFunctionType
    scratch = nc.dram_tensor("x_mid_scratch", (B * N, D), f32).ap()

    with ExitStack() as ctx:
        def sb(name, shape, dt=f32):
            return ctx.enter_context(nc.sbuf_tensor(name, shape, dt))

        def sem(name):
            return ctx.enter_context(nc.semaphore(name))

        early_sb = sb("early_sb", [128, width(EARLY)])
        net_sb = sb("net_sb", [128, width(NET)])
        att_sb = sb("att_sb", [128, width(ATT)])
        rows_sb = sb("rows_sb", [3, 4 * D])

        def E(name):
            return early_sb[:, EARLY[name][0]:EARLY[name][1]]

        def W(name, parts=128):
            return net_sb[0:parts, NET[name][0]:NET[name][1]]

        def A(name):
            return att_sb[:, ATT[name][0]:ATT[name][1]]

        def vec(name, parts=128):
            at = EARLY["vec"][0] + VEC[name]
            return early_sb[0:parts, at:at + 1]

        ident = E("ident")
        derived = sb("derived", [128, 4])
        half_b4, half_gb3, range_07, range_03 = (derived[:, i:i + 1] for i in range(4))
        minus_half = sb("minus_half", [128, GS])
        ones_bf = sb("ones_bf", [128, 128], bf16)
        row_rest = sb("row_rest", [3, 4 * D])
        row_hi = sb("row_hi", [3, 4 * D], bf16)
        row_mid = sb("row_mid", [3, 4 * D], bf16)
        row_lo = sb("row_lo", [3, 4 * D], bf16)
        row_pick = sb("row_pick", [3, 4 * D])
        row_part = sb("row_part", [3, 4 * D])
        bias_rows = sb("bias_rows", [128, 4 * D], bf16)

        x_in = sb("x_in", [128, SLOTS, D])
        x_mid = sb("x_mid", [128, SLOTS, D])
        x_att = sb("x_att", [128, SLOTS, D])
        x_out = sb("x_out", [128, SLOTS, D])
        ln = sb("ln", [128, SLOTS, D])
        tln = sb("tln", [128, SLOTS, D])
        lnT = sb("lnT", [128, SLOTS * D])
        pq = sb("pq", [128, SLOTS, 2, D])
        pre = sb("pre", [128, SLOTS, D])
        ln_sum = sb("ln_sum", [128, GROUPS, D])
        sum_half = sb("sum_half", [128, GROUPS, 2, D])
        stats = sb("stats", [128, 3 * GROUPS, GS, 6])
        small = sb("small", [128, 3 * GROUPS, 9, GS])
        h1 = sb("h1", [128, 2, GW])
        h2 = sb("h2", [128, 2, GW // 2])
        h3 = sb("h3", [128, 2, GW // 4])
        tf = sb("tf", [128, 2 * ITEMS, GS])
        coef = sb("coef", [128, 2 * GROUPS, 12, GS])
        gf = sb("gf", [128, 2, 8])
        g2x = sb("g2x", [32, 2, 128])
        alpha = sb("alpha", [128, 2])
        h1q = sb("h1q", [128, B, SLOTS, T])
        h1k = sb("h1k", [128, B, SLOTS, T])
        vT = sb("vT", [128, B, SLOTS, T])
        gate = sb("gate", [128, SLOTS, D])
        qk = sb("qk", [128, 8, GS, D])
        am = sb("am", [128, B, D])
        ai = sb("ai", [128, B, D])
        zr = sb("zr", [128, B, D])
        zi = sb("zi", [128, B, D])
        mix = sb("mix", [128, B, D])
        og = sb("og", [128, H, SLOTS, HD])
        ogT = sb("ogT", [128, H, D])

        bank = [ctx.enter_context(nc.psum_tensor(f"bank{i}", [128, 512], f32)) for i in range(8)]
        trans_ps = bank[0:2]
        pq_ps = bank[2:4]
        l2_ps, l3_ps, l4_ps, gf_ps = bank[4:8]

        x_loaded = [sem(f"x_loaded{g}") for g in range(GROUPS)]
        early_loaded, net_loaded, att_loaded, rows_loaded = (
            sem(n) for n in ("early_loaded", "net_loaded", "att_loaded", "rows_loaded"))
        x_mid_stored, x_att_loaded, out_stored = (sem(n) for n in ("x_mid_stored", "x_att_loaded", "out_stored"))
        consts_ready, signs_ready, bias_rows_ready, pool_step, dve_step = (
            sem(n) for n in ("consts_ready", "signs_ready", "bias_rows_ready", "pool_step", "dve_step"))
        stats_ready, rstd_ready, ln_ready, tln_ready, ln_sum_ready = (
            sem(n) for n in ("stats_ready", "rstd_ready", "ln_ready", "tln_ready", "ln_sum_ready"))
        trans_done, trans_read, pq_done, pq_lo_read, pq_hi_read = (
            sem(n) for n in ("trans_done", "trans_read", "pq_done", "pq_lo_read", "pq_hi_read"))
        pre_ready, l2_done, gelu2_done, l3_done, gelu3_done, l4_done, tanh_done = (
            sem(n) for n in ("pre_ready", "l2_done", "gelu2_done", "l3_done", "gelu3_done", "l4_done", "tanh_done"))
        gf_pe, gf_act, x_mid_ready, x_out_ready = (sem(n) for n in ("gf_pe", "gf_act", "x_mid_ready", "x_out_ready"))
        proj1_done, proj1_read, qk_done, exp_done, clamp_done, log_done, soft_done = (
            sem(n) for n in ("proj1_done", "proj1_read", "qk_done", "exp_done", "clamp_done", "log_done",
                             "soft_done"))
        a_done, am_ready, zsum_done, mix_ready, mixed_done, og_ready, proj_done, x_att_ready = (
            sem(n) for n in ("a_done", "am_ready", "zsum_done", "mix_ready", "mixed_done", "og_ready",
                             "proj_done", "x_att_ready"))

        def use_ln(f, g):
            return 24 * f + 2 * g

        def use_pre(f, s):
            return 24 * f + (2 * s + 1 if s < GROUPS else GROUPS + s)

        def use_ln_att(g):
            return 16 + g

        def use_og(hg):
            return 20 + hg

        LN_SRC = [x_in, x_mid, x_att]

        def group(t, g):
            return t[:, GS * g:GS * g + GS]

        block = ctx.enter_context(nc.Block())

        @block.sync
        def _(sp):
            x_v = x.rearrange("(p s) f -> p s f", p=128)
            for g in range(GROUPS):
                sp.dma_start(group(x_in, g), x_v[:, GS * g:GS * g + GS, :]).then_inc(x_loaded[g], 16)
            sp.dma_start(rows_sb[:, :], rows).then_inc(rows_loaded, 16)
            sp.dma_start(att_sb[:, :], att).then_inc(att_loaded, 16)
            s_v = scratch.rearrange("(p s) f -> p s f", p=128)
            for g in range(GROUPS):
                sp.wait_ge(x_mid_ready, g + 1)
                sp.dma_start(s_v[:, GS * g:GS * g + GS, :], group(x_mid, g)).then_inc(x_mid_stored, 16)
            sp.wait_ge(x_mid_stored, 16 * GROUPS)
            for b in range(B):
                sp.dma_start(x_att[T * b:T * b + T, :, :],
                             scratch[N * b:N * b + N, :].rearrange("(h t) f -> t h f", t=T)
                             ).then_inc(x_att_loaded, 16)
            for g in range(GROUPS):
                sp.wait_ge(x_out_ready, g + 1)
                for b in range(B):
                    dst = out[N * b + GS * T * g:N * b + GS * T * (g + 1), :].rearrange("(h t) f -> t h f", t=T)
                    sp.dma_start(dst, x_out[T * b:T * b + T, GS * g:GS * g + GS, :]).then_inc(out_stored, 16)
            sp.wait_ge(out_stored, 16 * GROUPS * B)

        @block.gpsimd
        def _(pool):
            steps = [0]

            def then(ins):
                steps[0] += 1
                ins.then_inc(pool_step, 1)
                pool.wait_ge(pool_step, steps[0])

            def rstd(n):
                st, o = stats[:, n], small[:, n]
                pool.wait_ge(stats_ready, n + 1)
                both = o[:, 0:2].rearrange("p k s -> p s k")
                then(nc.gpsimd.tensor_tensor(both, st[:, :, 1:3], st[:, :, 4:6], ALU.add))
                then(nc.gpsimd.tensor_tensor(o[:, 2], st[:, :, 1], st[:, :, 4], ALU.subtract))
                then(nc.gpsimd.tensor_tensor(o[:, 3], o[:, 2], o[:, 2], ALU.mult))
                then(nc.gpsimd.tensor_scalar(o[:, 4], o[:, 1], 4.0 / D, 4.0 * EPS, ALU.mult, ALU.add))
                then(nc.gpsimd.tensor_tensor(o[:, 5], o[:, 4], o[:, 3], ALU.add))
                then(nc.gpsimd.tensor_tensor(o[:, 6], o[:, 5], minus_half[:, :], ALU.pow))
                then(nc.gpsimd.tensor_tensor(o[:, 8], o[:, 6], o[:, 0], ALU.mult))
                nc.gpsimd.tensor_tensor(o[:, 7], o[:, 6], o[:, 6], ALU.add).then_inc(rstd_ready, 1)

            def sum_slots(f, g):
                pool.wait_ge(ln_ready, 8 * f + g + 1)
                src = group(ln, g)
                then(nc.gpsimd.tensor_tensor(sum_half[:, g], src[:, 0:2], src[:, 2:4], ALU.add))
                nc.gpsimd.tensor_tensor(ln_sum[:, g], sum_half[:, g, 0], sum_half[:, g, 1],
                                        ALU.add).then_inc(ln_sum_ready, 1)

            def twist(f, g):
                src = group(ln, g).rearrange("p s (q e) -> p s q e", q=4)
                dst = group(tln, g).rearrange("p s (q e) -> p s q e", q=4)
                nc.gpsimd.tensor_copy(dst[:, :, 0], src[:, :, 2])
                nc.gpsimd.tensor_copy(dst[:, :, 3], src[:, :, 1])
                nc.gpsimd.tensor_scalar(dst[:, :, 1], src[:, :, 3], -1.0, 0.0, ALU.mult, ALU.add)
                nc.gpsimd.tensor_scalar(dst[:, :, 2], src[:, :, 0], -1.0, 0.0, ALU.mult, ALU.add
                                        ).then_inc(tln_ready, 1)

            nc.gpsimd.memset(minus_half[:, :], -0.5)
            nc.gpsimd.memset(ones_bf[:, :], 1.0)
            then(nc.gpsimd.memset(bias_rows[:, :], 0.0))
            pool.wait_ge(early_loaded, 16)
            for p in (0, 96):
                m = early_sb[p:p + 32, EARLY["w1t"][0]:EARLY["w1t"][1]]
                ins = nc.gpsimd.tensor_scalar(m, m, -1.0, 0.0, ALU.mult, ALU.add)
                ins.then_inc(signs_ready, 1)
            pool.wait_ge(signs_ready, 2)
            rstd(0)
            nc.gpsimd.tensor_scalar(half_b4, vec("b4"), 0.5, 0.0, ALU.mult, ALU.add)
            nc.gpsimd.tensor_scalar(half_gb3, vec("gc3"), 0.5, 0.0, ALU.mult, ALU.add)
            nc.gpsimd.tensor_scalar(range_07, vec("range"), 0.7, 0.0, ALU.mult, ALU.add)
            nc.gpsimd.tensor_scalar(range_03, vec("range"), 0.3, 0.0, ALU.mult, ALU.add).then_inc(consts_ready, 1)
            for g in range(1, GROUPS):
                rstd(g)
                sum_slots(0, g - 1)
            sum_slots(0, GROUPS - 1)
            for g in range(GROUPS):
                twist(0, g)
            pool.wait_ge(rows_loaded, 16)
            then(nc.gpsimd.tensor_copy(row_hi[:, :], rows_sb[:, :]))
            then(nc.gpsimd.tensor_tensor(row_rest[:, :], rows_sb[:, :], row_hi[:, :], ALU.subtract))
            then(nc.gpsimd.tensor_copy(row_mid[:, :], row_rest[:, :]))
            then(nc.gpsimd.tensor_tensor(row_rest[:, :], row_rest[:, :], row_mid[:, :], ALU.subtract))
            then(nc.gpsimd.tensor_scalar(row_pick[:, :], row_hi[:, :], ident[0:3, 0:1], 0.0, ALU.mult, ALU.add))
            then(nc.gpsimd.tensor_scalar(row_part[:, :], row_mid[:, :], ident[0:3, 1:2], 0.0, ALU.mult, ALU.add))
            then(nc.gpsimd.tensor_tensor(row_pick[:, :], row_pick[:, :], row_part[:, :], ALU.add))
            then(nc.gpsimd.tensor_scalar(row_part[:, :], row_rest[:, :], ident[0:3, 2:3], 0.0, ALU.mult, ALU.add))
            nc.gpsimd.tensor_tensor(bias_rows[0:3, :], row_pick[:, :], row_part[:, :],
                                    ALU.add).then_inc(bias_rows_ready, 1)
            pool.wait_ge(bias_rows_ready, 1)
            for g in range(GROUPS):
                rstd(GROUPS + g)
            rstd(2 * GROUPS)
            for g in range(1, GROUPS):
                rstd(2 * GROUPS + g)
                sum_slots(1, g - 1)
            sum_slots(1, GROUPS - 1)
            for g in range(GROUPS):
                twist(1, g)

        @block.scalar
        def _(act):
            act.dma_start(early_sb[:, :], early).then_inc(early_loaded, 16)
            act.dma_start(net_sb[:, :], net).then_inc(net_loaded, 16)
            nc.scalar.preload_act_table_set("gelu_and_others")

            def take_transposed(use, dst, func=ACT.Identity, bias=0.0):
                act.wait_ge(trans_done, use + 1)
                nc.scalar.activation(dst, trans_ps[use % 2][:, :], func, bias=bias).then_inc(trans_read, 1)

            def gelu1(f, s):
                n = ITEMS * f + s
                if n >= 2:
                    act.wait_ge(l2_done, n - 1)
                take_transposed(use_pre(f, s), h1[:, n % 2], ACT.Gelu, vec("b1"))

            def gelu2(f, s):
                n = ITEMS * f + s
                act.wait_ge(l2_done, n + 1)
                if n >= 2:
                    act.wait_ge(l3_done, n - 1)
                nc.scalar.activation(h2[:, n % 2], l2_ps[:, 0:GW // 2], ACT.Gelu,
                                     bias=vec("b2")).then_inc(gelu2_done, 1)

            def gelu3(f, s):
                n = ITEMS * f + s
                act.wait_ge(l3_done, n + 1)
                if n >= 2:
                    act.wait_ge(l4_done, n - 1)
                nc.scalar.activation(h3[:, n % 2], l3_ps[:, 0:GW // 4], ACT.Gelu,
                                     bias=vec("b3")).then_inc(gelu3_done, 1)

            def tanh(f, s):
                n = ITEMS * f + s
                act.wait_ge(l4_done, n + 1)
                nc.scalar.activation(tf[:, n], l4_ps[:, 0:GS], ACT.Tanh, bias=half_b4, scale=0.5
                                     ).then_inc(tanh_done, 1)

            def context_step(f, k):
                act.wait_ge(gf_pe, 4 * f + k + 1)
                if k == 0:
                    ins = nc.scalar.activation(gf[:, f, 0:2], gf_ps[:, 0:2], ACT.Identity)
                elif k == 1:
                    ins = nc.scalar.activation(gf[0:64, f, 2:4], gf_ps[0:64, 8:10], ACT.Gelu, bias=vec("gc1", 64))
                elif k == 2:
                    wide = gf_ps[0:32, 16:18].unsqueeze(2).to_broadcast([32, B, T])
                    ins = nc.scalar.activation(g2x[:, f, :].rearrange("p (b t) -> p b t", b=B), wide, ACT.Gelu,
                                               bias=vec("gc2", 32))
                else:
                    ins = nc.scalar.activation(gf[:, f, 6:7], gf_ps[:, 24:25], ACT.Tanh, bias=half_gb3, scale=0.5)
                ins.then_inc(gf_act, 1)

            def ffn(f):
                for s in range(ITEMS + 3):
                    context = s == GROUPS
                    if context:
                        context_step(f, 0)
                    if s >= 3:
                        tanh(f, s - 3)
                    if context:
                        context_step(f, 1)
                    if 2 <= s < ITEMS + 2:
                        gelu3(f, s - 2)
                    if context:
                        context_step(f, 2)
                    if 1 <= s < ITEMS + 1:
                        gelu2(f, s - 1)
                    if context:
                        context_step(f, 3)
                    if s < GROUPS:
                        take_transposed(use_ln(f, s), lnT[:, GW * s:GW * s + GW])
                        act.wait_ge(pq_done, 2 * (GROUPS * f + s) + 2)
                        nc.scalar.activation(pq[:, GS * s + 2:GS * s + 4].rearrange("p s k e -> p (s k e)"),
                                             pq_ps[1][:, :], ACT.Identity).then_inc(pq_hi_read, 1)
                    if s < ITEMS:
                        gelu1(f, s)

            act.wait_ge(early_loaded, 16)
            act.wait_ge(consts_ready, 1)
            ffn(0)
            for g in range(GROUPS):
                take_transposed(use_ln_att(g), lnT[:, GW * g:GW * g + GW])
                for i, (dst, bias) in enumerate(((h1q, vec("q1")), (h1k, vec("k1")), (vT, vec("v")), (gate, 0.0))):
                    act.wait_ge(proj1_done, 4 * g + i + 1)
                    if i == 3:
                        d, src = group(dst, g).rearrange("p s e -> p (s e)"), bank[2 + i][:, :]
                    else:
                        d = dst[:, :, GS * g:GS * g + GS, :].rearrange("p b s t -> p s b t")
                        src = bank[2 + i][:, :].rearrange("p (s b t) -> p s b t", s=GS, b=B)
                    nc.scalar.activation(d, src, ACT.Gelu, bias=bias).then_inc(proj1_read, 1)
            nc.scalar.preload_act_table_set("natural_log_exp_and_others")
            for n in range(8 + 2):
                if n < 8:
                    act.wait_ge(qk_done, n + 1)
                    e = qk[:, n].rearrange("p s e -> p (s e)")
                    nc.scalar.activation(e, bank[2 + n % 4][:, :], ACT.Exp).then_inc(exp_done, 1)
                if n >= 2:
                    act.wait_ge(clamp_done, n - 1)
                    e = qk[:, n - 2].rearrange("p s e -> p (s e)")
                    nc.scalar.activation(e, e, ACT.Ln, bias=1.0).then_inc(log_done, 1)
            nc.scalar.preload_act_table_set("gelu_and_others")
            for hg in range(GROUPS):
                take_transposed(use_og(hg), group(ogT, hg).rearrange("p h e -> p (h e)"))
            ffn(1)

        @block.vector
        def _(dve):
            steps = [0]

            def then(ins):
                steps[0] += 1
                ins.then_inc(dve_step, 1)
                dve.wait_ge(dve_step, steps[0])

            def bn_stats(n):
                layer, g = divmod(n, GROUPS)
                if layer == 0:
                    dve.wait_ge(x_loaded[g], 16)
                else:
                    dve.wait_ge((x_mid_ready, x_att_ready)[layer - 1], g + 1)
                for j in range(GS):
                    last = nc.vector.bn_stats(stats[:, n, j], LN_SRC[layer][:, GS * g + j])
                last.then_inc(stats_ready, 1)

            def normalise(n):
                layer, g = divmod(n, GROUPS)
                dve.wait_ge(rstd_ready, n + 1)
                for j in range(GS):
                    last = nc.vector.tensor_scalar(ln[:, GS * g + j], LN_SRC[layer][:, GS * g + j],
                                                   small[:, n, 7, j:j + 1], small[:, n, 8, j:j + 1],
                                                   ALU.mult, ALU.subtract)
                last.then_inc(ln_ready, 1)

            def take_pq(f, g):
                dve.wait_ge(pq_done, 2 * (GROUPS * f + g) + 1)
                nc.vector.tensor_copy(pq[:, GS * g:GS * g + 2].rearrange("p s k e -> p (s k e)"),
                                      pq_ps[0][:, :]).then_inc(pq_lo_read, 1)

            def cf(f, g, a, b=None):
                c = coef[:, GROUPS * f + g]
                return c[:, a] if b is None else c[:, a:b]

            def coupling(f, s, row):
                n = ITEMS * f + s
                dve.wait_ge(tanh_done, n + 1)
                then(nc.vector.tensor_scalar(cf(f, s % GROUPS, row), tf[:, n], range_03, alpha[:, f:f + 1],
                                             ALU.mult, ALU.add))

            def update(f, s):
                cycle, g = divmod(s, GROUPS)
                if cycle == 1:
                    coupling(f, s - GROUPS, 0)
                    for j in range(GS):
                        at = GS * g + j
                        last = nc.vector.scalar_tensor_tensor(
                            pre[:, at], pq[:, at, 1], cf(f, g, 0)[:, j:j + 1], pq[:, at, 0], ALU.mult, ALU.add)
                else:
                    coupling(f, s - GROUPS, 1)
                    nc.vector.tensor_tensor(cf(f, g, 2), cf(f, g, 0), cf(f, g, 1), ALU.mult)
                    then(nc.vector.tensor_tensor(cf(f, g, 4), cf(f, g, 0), cf(f, g, 1), ALU.add))
                    then(nc.vector.tensor_scalar(cf(f, g, 3), cf(f, g, 2), -1.0, 1.0, ALU.mult, ALU.add))
                    for j in range(GS):
                        at = GS * g + j
                        last = nc.vector.tensor_scalar(pre[:, at], pq[:, at, 0], cf(f, g, 3)[:, j:j + 1], None,
                                                       ALU.mult)
                    then(last)
                    for j in range(GS):
                        at = GS * g + j
                        last = nc.vector.scalar_tensor_tensor(
                            pre[:, at], pq[:, at, 1], cf(f, g, 4)[:, j:j + 1], pre[:, at], ALU.mult, ALU.add)
                last.then_inc(pre_ready, 1)

            def finish(f, g):
                src, dst = ((x_in, x_mid), (x_att, x_out))[f]
                nc.vector.tensor_scalar(cf(f, g, 5, 7), cf(f, g, 3, 5), 0.5, None, ALU.mult)
                coupling(f, 2 * GROUPS + g, 7)
                nc.vector.tensor_tensor(cf(f, g, 8), cf(f, g, 6), cf(f, g, 7), ALU.mult)
                then(nc.vector.tensor_tensor(cf(f, g, 9), cf(f, g, 5), cf(f, g, 7), ALU.mult))
                nc.vector.tensor_tensor(cf(f, g, 10), cf(f, g, 5), cf(f, g, 8), ALU.subtract)
                then(nc.vector.tensor_tensor(cf(f, g, 11), cf(f, g, 6), cf(f, g, 9), ALU.add))
                for j in range(GS):
                    at = GS * g + j
                    last = nc.vector.scalar_tensor_tensor(
                        dst[:, at], ln[:, at], cf(f, g, 10)[:, j:j + 1], src[:, at], ALU.mult, ALU.add)
                then(last)
                dve.wait_ge(tln_ready, GROUPS * f + g + 1)
                for j in range(GS):
                    at = GS * g + j
                    last = nc.vector.scalar_tensor_tensor(
                        dst[:, at], tln[:, at], cf(f, g, 11)[:, j:j + 1], dst[:, at], ALU.mult, ALU.add)
                last.then_inc((x_mid_ready, x_out_ready)[f], 1)

            def ffn_cycles(f):
                dve.wait_ge(consts_ready, 1)
                dve.wait_ge(gf_act, 4 * f + 4)
                then(nc.vector.tensor_scalar(alpha[:, f:f + 1], gf[:, f, 6:7], range_07, BASE_COUPLING,
                                             ALU.mult, ALU.add))
                for s in range(GROUPS, ITEMS):
                    update(f, s)

            bn_stats(0)
            bn_stats(1)
            for g in range(GROUPS):
                normalise(g)
                if g + 2 < GROUPS:
                    bn_stats(g + 2)
                if g >= 1:
                    take_pq(0, g - 1)
            take_pq(0, GROUPS - 1)
            ffn_cycles(0)
            for g in range(GROUPS):
                finish(0, g)
                bn_stats(GROUPS + g)
                if g >= 1:
                    normalise(GROUPS + g - 1)
            normalise(2 * GROUPS - 1)

            def mix_first(b):
                dve.wait_ge(a_done, b + 1)
                nc.vector.tensor_tensor(am[:, b], bank[6 + b][:, 0:D], A("mask"), ALU.mult).then_inc(am_ready, 1)

            def mix_second(b):
                dve.wait_ge(zsum_done, b + 1)
                nc.vector.tensor_scalar(zr[:, b], bank[6 + b][:, D:2 * D], float(D), None, ALU.add)
                dve.wait_ge(am_ready, b + 1)
                then(nc.vector.tensor_tensor(ai[:, b], am[:, b], ident, ALU.add))
                then(nc.vector.reciprocal(zi[:, b], zr[:, b]))
                nc.vector.tensor_tensor(mix[:, b], ai[:, b], zi[:, b], ALU.mult).then_inc(mix_ready, 1)

            dve.wait_ge(att_loaded, 16)
            for n in range(8 + 3):
                if n >= 3:
                    dve.wait_ge(log_done, n - 2)
                    e = qk[:, n - 3].rearrange("p s e -> p (s e)")
                    nc.vector.tensor_tensor(e, e, bank[2 + (n - 3) % 4][:, :], ALU.max).then_inc(soft_done, 1)
                if n < 8:
                    dve.wait_ge(exp_done, n + 1)
                    e = qk[:, n].rearrange("p s e -> p (s e)")
                    nc.vector.tensor_scalar(e, e, EXP_TOP, None, ALU.min).then_inc(clamp_done, 1)
                if n == 8:
                    mix_first(0)
                if n == 9:
                    mix_second(0)
            mix_first(1)
            mix_second(1)
            for g in range(GROUPS):
                dve.wait_ge(mixed_done, g + 1)
                nc.vector.tensor_tensor(og[:, :, GS * g:GS * g + GS, :].rearrange("p h j n -> p j h n"),
                                        bank[2 + g][:, :].rearrange("p (j h n) -> p j h n", j=GS, h=H),
                                        group(gate, g).rearrange("p j (h n) -> p j h n", h=H),
                                        ALU.mult).then_inc(og_ready, 1)
            dve.wait_ge(x_att_loaded, 16 * B)
            for hg in range(GROUPS):
                dve.wait_ge(proj_done, hg + 1)
                r = group(x_att, hg).rearrange("p h e -> p (h e)")
                nc.vector.tensor_tensor(r, bank[2 + hg][:, :], r, ALU.add).then_inc(x_att_ready, 1)
                bn_stats(2 * GROUPS + hg)
                if hg >= 1:
                    normalise(2 * GROUPS + hg - 1)
                if hg >= 2:
                    take_pq(1, hg - 2)
            normalise(3 * GROUPS - 1)
            take_pq(1, GROUPS - 2)
            take_pq(1, GROUPS - 1)
            ffn_cycles(1)
            for g in range(GROUPS):
                finish(1, g)

        @block.tensor
        def _(pe):
            def transpose_group(use, tiles):
                if use >= 2:
                    pe.wait_ge(trans_read, use - 1)
                for j, tile in enumerate(tiles):
                    last = nc.tensor.transpose(trans_ps[use % 2][:, D * j:D * j + D], tile, ident)
                last.then_inc(trans_done, 1)

            def transpose_ln(layer, g, use):
                pe.wait_ge(ln_ready, GROUPS * layer + g + 1)
                transpose_group(use, [ln[:, GS * g + j] for j in range(GS)])

            def products_pq(f, g):
                pe.wait_ge(trans_read, use_ln(f, g) + 1)
                for half, read in ((0, pq_lo_read), (1, pq_hi_read)):
                    if f or g:
                        pe.wait_ge(read, GROUPS * f + g)
                    for j in range(2):
                        at = D * (GS * g + 2 * half + j)
                        last = nc.tensor.matmul(pq_ps[half][:, 2 * D * j:2 * D * (j + 1)], lnT[:, at:at + D],
                                                early_sb[:, EARLY["w1"][0]:EARLY["w1t"][1]],
                                                start=True, stop=True)
                    last.then_inc(pq_done, 1)

            def transpose_pre(f, s):
                cycle, g = divmod(s, GROUPS)
                if cycle == 0:
                    pe.wait_ge(pq_lo_read, GROUPS * f + g + 1)
                    pe.wait_ge(pq_hi_read, GROUPS * f + g + 1)
                    tiles = [pq[:, GS * g + j, 0] for j in range(GS)]
                else:
                    pe.wait_ge(pre_ready, 2 * GROUPS * f + s - GROUPS + 1)
                    tiles = [pre[:, GS * g + j] for j in range(GS)]
                transpose_group(use_pre(f, s), tiles)

            def layer2(f, s):
                n = ITEMS * f + s
                pe.wait_ge(trans_read, use_pre(f, s) + 1)
                if n:
                    pe.wait_ge(gelu2_done, n)
                if n == ITEMS:
                    pe.wait_ge(x_att_ready, 3)
                for half in range(2):
                    last = nc.tensor.matmul(l2_ps[64 * half:64 * half + 64, 0:GW // 2], W("w2"),
                                            h1[:, n % 2, GW // 2 * half:GW // 2 * (half + 1)],
                                            start=True, stop=True)
                last.then_inc(l2_done, 1)

            def layer3(f, s):
                n = ITEMS * f + s
                pe.wait_ge(gelu2_done, n + 1)
                if n:
                    pe.wait_ge(gelu3_done, n)
                if n == ITEMS:
                    pe.wait_ge(x_att_ready, 4)
                for half in range(2):
                    last = nc.tensor.matmul(l3_ps[64 * half:64 * half + 64, 0:D], W("w3"),
                                            h2[:, n % 2, D * half:D * half + D], start=True, stop=True)
                last.then_inc(l3_done, 1)

            def layer4(f, s):
                n = ITEMS * f + s
                pe.wait_ge(gelu3_done, n + 1)
                if n:
                    pe.wait_ge(tanh_done, n)
                nc.tensor.matmul(l4_ps[:, 0:GS], h3[:, n % 2], W("w4"), start=True, stop=True).then_inc(l4_done, 1)

            def context_step(f, k):
                if k == 0:
                    for g in range(GROUPS):
                        pe.wait_ge(ln_sum_ready, GROUPS * f + g + 1)
                        ins = nc.tensor.matmul(gf_ps[:, 0:2], ln_sum[:, g], E("sel"),
                                               start=(g == 0), stop=(g == GROUPS - 1))
                else:
                    pe.wait_ge(gf_act, 4 * f + k)
                    if k == 1:
                        ins = nc.tensor.matmul(gf_ps[0:64, 8:10], W("gc1"), gf[:, f, 0:2], start=True, stop=True)
                    elif k == 2:
                        ins = nc.tensor.matmul(gf_ps[0:32, 16:18], W("gc2", 64), gf[0:64, f, 2:4],
                                               start=True, stop=True)
                    else:
                        ins = nc.tensor.matmul(gf_ps[:, 24:25], g2x[:, f], W("gc3", 32), start=True, stop=True)
                ins.then_inc(gf_pe, 1)

            def ffn(f):
                for s in range(ITEMS + 3):
                    context = s == GROUPS
                    if context:
                        context_step(f, 0)
                    if s >= 3:
                        layer4(f, s - 3)
                    if context:
                        context_step(f, 1)
                    if 2 <= s < ITEMS + 2:
                        layer3(f, s - 2)
                    if context:
                        context_step(f, 2)
                    if 1 <= s < ITEMS + 1:
                        layer2(f, s - 1)
                    if context:
                        context_step(f, 3)
                    if s < GROUPS:
                        transpose_ln(2 * f, s, use_ln(f, s))
                        products_pq(f, s)
                    if s < ITEMS:
                        transpose_pre(f, s)

            def biased(dst, row, tiles, weights):
                bias = bias_rows[:, D * ROWS[row]:D * ROWS[row] + D].unsqueeze(1).to_broadcast([128, GS, D])
                nc.tensor.matmul(dst[:, :].rearrange("p (j e) -> p j e", j=GS), ones_bf[:, :], bias,
                                 start=True, stop=False, skip_group_check=True)
                for j, tile in enumerate(tiles):
                    last = nc.tensor.matmul(dst[:, D * j:D * j + D], tile, weights, start=False,
                                            stop=(j == GS - 1), skip_group_check=True)
                return last

            pe.wait_ge(early_loaded, 16)
            pe.wait_ge(net_loaded, 16)
            pe.wait_ge(signs_ready, 2)
            ffn(0)
            pe.wait_ge(gelu2_done, ITEMS)
            pe.wait_ge(gelu3_done, ITEMS)
            pe.wait_ge(att_loaded, 16)
            pe.wait_ge(bias_rows_ready, 1)
            for g in range(GROUPS):
                transpose_ln(1, g, use_ln_att(g))
                pe.wait_ge(trans_read, use_ln_att(g) + 1)
                for i, name in enumerate(("q1", "k1", "v")):
                    if g:
                        pe.wait_ge(proj1_read, 4 * (g - 1) + i + 1)
                    nc.tensor.matmul(bank[2 + i][:, :], A(name), lnT[:, GW * g:GW * g + GW],
                                     start=True, stop=True).then_inc(proj1_done, 1)
                if g:
                    pe.wait_ge(proj1_read, 4 * g)
                biased(bank[5], "g", [lnT[:, D * (GS * g + j):D * (GS * g + j + 1)] for j in range(GS)],
                       A("g")).then_inc(proj1_done, 1)

            def softplus_inputs(i):
                b, u = divmod(i, 2)
                for x_, (h, row) in enumerate(((h1q, "q2"), (h1k, "k2"))):
                    n = 2 * i + x_
                    if i < 2:
                        pe.wait_ge(proj1_read, 4 * (GROUPS - 1) + n + 1)
                    else:
                        pe.wait_ge(soft_done, n - 3)
                    tiles = [h[:, b, 8 * u + 2 * j:8 * u + 2 * j + 2, :].rearrange("p s t -> p (s t)")
                             for j in range(GS)]
                    biased(bank[2 + n % 4], row, tiles, A(row)).then_inc(qk_done, 1)

            def product_qk(i):
                b, u = divmod(i, 2)
                pe.wait_ge(soft_done, 2 * i + 2)
                if i == 0:
                    pe.wait_ge(tanh_done, ITEMS)
                for j in range(GS):
                    last = nc.tensor.matmul(bank[6 + b][:, 0:D], qk[:, 2 * i + 1, j], qk[:, 2 * i, j],
                                            start=(u == 0 and j == 0), stop=(u == 1 and j == GS - 1))
                if u == 1:
                    last.then_inc(a_done, 1)

            def z_sum(b):
                pe.wait_ge(am_ready, b + 1)
                nc.tensor.matmul(bank[6 + b][:, D:2 * D], A("ones"), am[:, b], start=True,
                                 stop=True).then_inc(zsum_done, 1)

            softplus_inputs(0)
            softplus_inputs(1)
            product_qk(0)
            softplus_inputs(2)
            product_qk(1)
            softplus_inputs(3)
            z_sum(0)
            product_qk(2)
            product_qk(3)
            z_sum(1)
            for g in range(GROUPS):
                pe.wait_ge(soft_done, 4 + g + 1)
                for b in range(B):
                    pe.wait_ge(mix_ready, b + 1)
                    for j in range(GS):
                        last = nc.tensor.matmul(bank[2 + g][T * b:T * b + T, D * j:D * j + D],
                                                vT[:, b, GS * g + j, :], mix[:, b], start=True, stop=True)
                last.then_inc(mixed_done, 1)
            pe.wait_ge(og_ready, GROUPS)
            for hg in range(GROUPS):
                transpose_group(use_og(hg), [og[:, GS * hg + j].rearrange("p j n -> p (j n)") for j in range(GS)])
                pe.wait_ge(trans_read, use_og(hg) + 1)
                biased(bank[2 + hg], "p", [ogT[:, GS * hg + j] for j in range(GS)], A("p")).then_inc(proj_done, 1)
            pe.wait_ge(x_att_ready, 2)
            ffn(1)


def kernel(**inputs):
    import numpy as np
    import concourse.bacc as bacc
    from concourse import mybir as mb
    from concourse.bass_utils import run_bass_kernel_spmd

    a = {k.replace("L0_", "", 1): np.asarray(v) for k, v in inputs.items()}
    early = np.zeros((128, width(EARLY)), np.float32)
    net = np.zeros((128, width(NET)), np.float32)
    att = np.zeros((128, width(ATT)), np.float32)

    def put(dst, table, name, value, row=0, col=0):
        c = table[name][0] + col
        dst[row:row + value.shape[0], c:c + value.shape[1]] = value

    put(early, EARLY, "ident", np.eye(128, dtype=np.float32))
    w1 = a["ffn_cn_w1"]
    put(early, EARLY, "w1", w1)
    put(early, EARLY, "w1t", np.concatenate([w1[64:96], w1[96:128], w1[0:32], w1[32:64]]))
    for b in range(B):
        early[T * b:T * b + T, EARLY["sel"][0] + b] = 1.0 / N
    columns = dict(b1=(a["ffn_cn_b1"], 1), b2=(a["ffn_cn_b2"], 2), b3=(a["ffn_cn_b3"], 4),
                   q1=(a["attn_q_b1"], 1), k1=(a["attn_k_b1"], 1), v=(a["attn_v_b"], 1), b4=(a["ffn_cn_b4"], 128),
                   gc1=(a["ffn_gc_b1"], 1), gc2=(a["ffn_gc_b2"], 1), gc3=(a["ffn_gc_b3"], 128),
                   range=(a["ffn_adaptive_range"], 128))
    for name, (value, times) in columns.items():
        v = np.tile(value, times)
        early[0:v.shape[0], EARLY["vec"][0] + VEC[name]] = v
    put(net, NET, "w2", a["ffn_cn_w2"])
    for i in range(2):
        put(net, NET, "w3", a["ffn_cn_w3"], 64 * i, 32 * i)
    for i, slot in enumerate((0, 2, 1, 3)):
        put(net, NET, "w4", a["ffn_cn_w4"], 32 * i, slot)
    for i in (1, 2, 3):
        put(net, NET, f"gc{i}", a[f"ffn_gc_w{i}"])
    for name, key in dict(q1="q_w1", k1="k_w1", v="v_w", g="g_w", q2="q_w2", k2="k_w2", p="p_w").items():
        put(att, ATT, name, a["attn_" + key].T)
    put(att, ATT, "mask", np.kron(np.eye(H), np.full((HD, HD), SCALE)).astype(np.float32))
    put(att, ATT, "ones", np.ones((128, 128), np.float32))
    rows = np.tile(np.concatenate([a["attn_g_b"], a["attn_q_b2"], a["attn_k_b2"], a["attn_p_b"]])[None], (3, 1))
    arrays = dict(x=np.ascontiguousarray(a["attn_x"].reshape(B * N, D)), early=early, net=net, att=att,
                  rows=np.ascontiguousarray(rows))

    nc = bacc.Bacc("TRN2", target_bir_lowering=False, num_devices=1)
    args = [nc.dram_tensor(f"in_{k}", v.shape, mb.dt.from_np(v.dtype), kind="ExternalInput").ap()
            for k, v in arrays.items()]
    out = nc.dram_tensor("out_x", (B * N, D), mb.dt.float32, kind="ExternalOutput").ap()
    build(nc, *args, out)
    r = run_bass_kernel_spmd(nc, [{f"in_{k}": v for k, v in arrays.items()}], core_ids=[0])
    return r.results[0]["out_x"].reshape(B, N, D)
```

```python
import concourse.bass as bass
import concourse.mybir as mybir
from concourse.alu_op_type import AluOpType as ALU
from contextlib import ExitStack

B, N, D, H = 2, 1024, 128, 16
HD = D // H
SLOTS = B * N // D
T = N // SLOTS
GROUPS, GS = 4, SLOTS // 4
GW = GS * D
CYCLES = 3
ITEMS = CYCLES * GROUPS
SCALE = HD ** -0.5
EPS = 1e-5
EXP_TOP = 2.0 ** 60
BASE_COUPLING = 0.1

EARLY = dict(ident=(0, 128), w1=(128, 256), w1t=(256, 384), vec=(384, 400), sel=(400, 402))
NET = dict(w2=(0, 64), w3=(64, 128), w4=(128, 132), gc1=(132, 196), gc2=(196, 228), gc3=(228, 229))
ATT = dict(q1=(0, 128), k1=(128, 256), v=(256, 384), g=(384, 512), q2=(512, 640), k2=(640, 768),
           p=(768, 896), mask=(896, 1024), ones=(1024, 1152))
C1, C2, PROD, SUM, AB2, TURN2, BASE, DIR, PART, AB3 = 0, 1, 2, 3, 4, 6, 8, 10, 12, 14
VEC = dict(b1=0, b2=1, b3=2, q1=3, k1=4, v=5, b4=6, gc1=7, gc2=8, gc3=9, range=10)
ROWS = dict(g=0, q2=1, k2=2, p=3)


def width(table):
    return max(end for _, end in table.values())


def build(nc, x, early, net, att, rows, out):
    f32, bf16 = mybir.dt.float32, mybir.dt.bfloat16
    ACT = mybir.ActivationFunctionType
    scratch = nc.dram_tensor("x_mid_scratch", (B * N, D), f32).ap()

    with ExitStack() as ctx:
        def sb(name, shape, dt=f32):
            return ctx.enter_context(nc.sbuf_tensor(name, shape, dt))

        def sem(name):
            return ctx.enter_context(nc.semaphore(name))

        early_sb = sb("early_sb", [128, width(EARLY)])
        net_sb = sb("net_sb", [128, width(NET)])
        att_sb = sb("att_sb", [128, width(ATT)])
        rows_sb = sb("rows_sb", [3, 4 * D])

        def E(name):
            return early_sb[:, EARLY[name][0]:EARLY[name][1]]

        def W(name, parts=128):
            return net_sb[0:parts, NET[name][0]:NET[name][1]]

        def A(name):
            return att_sb[:, ATT[name][0]:ATT[name][1]]

        def vec(name, parts=128):
            at = EARLY["vec"][0] + VEC[name]
            return early_sb[0:parts, at:at + 1]

        ident = E("ident")
        derived = sb("derived", [128, 4])
        half_b4, half_gb3, range_07, range_03 = (derived[:, i:i + 1] for i in range(4))
        minus_half = sb("minus_half", [128, GS])
        ones_bf = sb("ones_bf", [128, 128], bf16)
        row_rest = sb("row_rest", [3, 4 * D])
        row_hi = sb("row_hi", [3, 4 * D], bf16)
        row_mid = sb("row_mid", [3, 4 * D], bf16)
        row_lo = sb("row_lo", [3, 4 * D], bf16)
        row_pick = sb("row_pick", [3, 4 * D])
        row_part = sb("row_part", [3, 4 * D])
        bias_rows = sb("bias_rows", [128, 4 * D], bf16)

        x_in = sb("x_in", [128, SLOTS, D])
        x_mid = sb("x_mid", [128, SLOTS, D])
        x_att = sb("x_att", [128, SLOTS, D])
        x_out = sb("x_out", [128, SLOTS, D])
        ln = sb("ln", [128, SLOTS, D])
        tln = sb("tln", [128, SLOTS, D])
        lnT = sb("lnT", [128, SLOTS * D])
        pq = sb("pq", [128, SLOTS, 2, D])
        pre = sb("pre", [128, SLOTS, D])
        rot = sb("rot", [128, SLOTS, D])
        token_sum = sb("token_sum", [128, 2, GROUPS, B])
        stats = sb("stats", [128, 3 * GROUPS, GS, 6])
        moments = sb("moments", [128, 3 * GROUPS, GS, 2])
        small = sb("small", [128, 3 * GROUPS, 4, GS])
        h1 = sb("h1", [128, 2, GW])
        h2 = sb("h2", [128, 2, GW // 2])
        h3 = sb("h3", [128, 2, GW // 4])
        tf = sb("tf", [128, 2 * ITEMS, GS])
        coef = sb("coef", [128, 2, 16, GROUPS, GS])
        gf = sb("gf", [128, 2, 8])
        g2x = sb("g2x", [32, 2, 128])
        alpha = sb("alpha", [128, 2])
        h1q = sb("h1q", [128, B, SLOTS, T])
        h1k = sb("h1k", [128, B, SLOTS, T])
        vT = sb("vT", [128, B, SLOTS, T])
        gate = sb("gate", [128, SLOTS, D])
        qk = sb("qk", [128, 8, GS, D])
        am = sb("am", [128, B, D])
        ai = sb("ai", [128, B, D])
        zr = sb("zr", [128, B, D])
        zi = sb("zi", [128, B, D])
        mix = sb("mix", [128, B, D])
        og = sb("og", [128, H, SLOTS, HD])
        ogT = sb("ogT", [128, H, D])

        bank = [ctx.enter_context(nc.psum_tensor(f"bank{i}", [128, 512], f32)) for i in range(8)]
        trans_ps = bank[0:2]
        pq_ps = bank[2:4]
        l2_ps, l3_ps, l4_ps, gf_ps = bank[4:8]
        soft_ps = bank[2:6] + bank[0:2]

        x_loaded = [sem(f"x_loaded{g}") for g in range(GROUPS)]
        early_loaded, net_loaded, att_loaded, rows_loaded = (
            sem(n) for n in ("early_loaded", "net_loaded", "att_loaded", "rows_loaded"))
        x_mid_stored, x_att_loaded, out_stored = (sem(n) for n in ("x_mid_stored", "x_att_loaded", "out_stored"))
        ones_ready, consts_ready, signs_ready, bias_rows_ready, pool_step, dve_step = (
            sem(n) for n in ("ones_ready", "consts_ready", "signs_ready", "bias_rows_ready", "pool_step", "dve_step"))
        alpha_ready, terms_ready, straight_ready = (sem(n) for n in ("alpha_ready", "terms_ready", "straight_ready"))
        stats_ready, moments_ready, rstd_ready, ln_ready, tln_ready = (
            sem(n) for n in ("stats_ready", "moments_ready", "rstd_ready", "ln_ready", "tln_ready"))
        trans_done, trans_read, pq_done, pq_read = (
            sem(n) for n in ("trans_done", "trans_read", "pq_done", "pq_read"))
        coupling_ready, rot_ready, finish_coef_ready, twisted_ready = (
            sem(n) for n in ("coupling_ready", "rot_ready", "finish_coef_ready", "twisted_ready"))
        pre_ready, l2_done, gelu2_done, l3_done, gelu3_done, l4_done, tanh_done = (
            sem(n) for n in ("pre_ready", "l2_done", "gelu2_done", "l3_done", "gelu3_done", "l4_done", "tanh_done"))
        gf_pe, gf_act, x_mid_ready, x_out_ready = (sem(n) for n in ("gf_pe", "gf_act", "x_mid_ready", "x_out_ready"))
        proj1_done, proj1_read, qk_done, exp_done, clamp_done, log_done, soft_done = (
            sem(n) for n in ("proj1_done", "proj1_read", "qk_done", "exp_done", "clamp_done", "log_done",
                             "soft_done"))
        a_done, am_ready, zsum_done, mix_ready, mixed_done, og_ready, proj_done, x_att_ready = (
            sem(n) for n in ("a_done", "am_ready", "zsum_done", "mix_ready", "mixed_done", "og_ready",
                             "proj_done", "x_att_ready"))

        def use_ln(f, g):
            return 24 * f + (0, 1, 3, 5)[g]

        def use_pre(f, s):
            return 24 * f + ((2, 4, 6, 7)[s] if s < GROUPS else GROUPS + s)

        def use_ln_att(g):
            return 16 + g

        def use_og(hg):
            return 20 + hg

        LN_SRC = [x_in, x_mid, x_att]

        def group(t, g):
            return t[:, GS * g:GS * g + GS]

        block = ctx.enter_context(nc.Block())

        @block.sync
        def _(sp):
            x_v = x.rearrange("(p s) f -> p s f", p=128)
            for g in range(GROUPS):
                sp.dma_start(group(x_in, g), x_v[:, GS * g:GS * g + GS, :]).then_inc(x_loaded[g], 16)
            sp.dma_start(rows_sb[:, :], rows).then_inc(rows_loaded, 16)
            sp.dma_start(att_sb[:, :], att).then_inc(att_loaded, 16)
            s_v = scratch.rearrange("(p s) f -> p s f", p=128)
            for g in range(GROUPS):
                sp.wait_ge(x_mid_ready, g + 1)
                sp.dma_start(s_v[:, GS * g:GS * g + GS, :], group(x_mid, g)).then_inc(x_mid_stored, 16)
            sp.wait_ge(x_mid_stored, 16 * GROUPS)
            for b in range(B):
                sp.dma_start(x_att[T * b:T * b + T, :, :],
                             scratch[N * b:N * b + N, :].rearrange("(h t) f -> t h f", t=T)
                             ).then_inc(x_att_loaded, 16)
            for g in range(GROUPS):
                sp.wait_ge(x_out_ready, g + 1)
                for b in range(B):
                    dst = out[N * b + GS * T * g:N * b + GS * T * (g + 1), :].rearrange("(h t) f -> t h f", t=T)
                    sp.dma_start(dst, x_out[T * b:T * b + T, GS * g:GS * g + GS, :]).then_inc(out_stored, 16)
            sp.wait_ge(out_stored, 16 * GROUPS * B)

        @block.gpsimd
        def _(pool):
            steps = [0]

            def then(ins):
                steps[0] += 1
                ins.then_inc(pool_step, 1)
                pool.wait_ge(pool_step, steps[0])

            def rstd(n):
                mv, o = moments[:, n], small[:, n]
                pool.wait_ge(moments_ready, n + 1)
                nc.gpsimd.tensor_scalar(o[:, 0], mv[:, :, 0], -1.0, 0.0, ALU.mult, ALU.add)
                then(nc.gpsimd.tensor_scalar(o[:, 1], mv[:, :, 1], 1.0, EPS, ALU.mult, ALU.add))
                then(nc.gpsimd.tensor_tensor(o[:, 2], o[:, 1], minus_half[:, :], ALU.pow))
                nc.gpsimd.tensor_tensor(o[:, 3], o[:, 2], o[:, 0], ALU.mult).then_inc(rstd_ready, 1)

            def rotate(f, g):
                pool.wait_ge(coupling_ready, 2 * GROUPS * f + g + 1)
                for j in range(GS):
                    at = GS * g + j
                    last = nc.gpsimd.tensor_scalar(rot[:, at], pq[:, at, 0], coef[:, f, C1, g, j:j + 1],
                                                   -1.0, ALU.mult, ALU.mult)
                then(last)
                nc.gpsimd.tensor_tensor(group(rot, g), group(rot, g), group(pq, g)[:, :, 1],
                                        ALU.add).then_inc(rot_ready, 1)

            def finish_terms(f):
                def rows(first, count=1):
                    return coef[:, f, first:first + count].rearrange("p r g j -> p r (g j)")

                pool.wait_ge(coupling_ready, 2 * GROUPS * (f + 1))
                pool.wait_ge(alpha_ready, f + 1)
                nc.gpsimd.tensor_tensor(rows(PROD), rows(C1), rows(C2), ALU.mult)
                then(nc.gpsimd.tensor_tensor(rows(SUM), rows(C1), rows(C2), ALU.add))
                for row, src, by, plus in ((AB2, PROD, -0.5, 0.5), (AB2 + 1, SUM, 0.5, 0.0),
                                           (TURN2, SUM, -0.5, 0.0), (TURN2 + 1, PROD, -0.5, 0.5)):
                    last = nc.gpsimd.tensor_scalar(rows(row), rows(src), by, plus, ALU.mult, ALU.add)
                then(last)
                nc.gpsimd.tensor_scalar(rows(DIR, 2), rows(TURN2, 2), range_03, 0.0, ALU.mult, ALU.add)
                then(nc.gpsimd.tensor_scalar(rows(BASE, 2), rows(TURN2, 2), alpha[:, f:f + 1], 0.0,
                                             ALU.mult, ALU.add))
                nc.gpsimd.tensor_tensor(rows(BASE, 2), rows(BASE, 2), rows(AB2, 2),
                                        ALU.add).then_inc(terms_ready, 1)

            def scale_twisted(f, g):
                pool.wait_ge(tln_ready, GROUPS * f + g + 1)
                pool.wait_ge(finish_coef_ready, GROUPS * f + g + 1)
                for j in range(GS):
                    t = tln[:, GS * g + j]
                    last = nc.gpsimd.tensor_scalar(t, t, coef[:, f, AB3 + 1, g, j:j + 1], 0.0,
                                                   ALU.mult, ALU.add)
                last.then_inc(twisted_ready, 1)

            nc.gpsimd.memset(minus_half[:, :], -0.5)
            nc.gpsimd.memset(ones_bf[:, :], 1.0).then_inc(ones_ready, 1)
            then(nc.gpsimd.memset(bias_rows[:, :], 0.0))
            for g in range(GROUPS):
                rstd(g)
            pool.wait_ge(rows_loaded, 16)
            pool.wait_ge(early_loaded, 16)
            then(nc.gpsimd.tensor_copy(row_hi[:, :], rows_sb[:, :]))
            then(nc.gpsimd.tensor_tensor(row_rest[:, :], rows_sb[:, :], row_hi[:, :], ALU.subtract))
            then(nc.gpsimd.tensor_copy(row_mid[:, :], row_rest[:, :]))
            then(nc.gpsimd.tensor_tensor(row_rest[:, :], row_rest[:, :], row_mid[:, :], ALU.subtract))
            then(nc.gpsimd.tensor_scalar(row_pick[:, :], row_hi[:, :], ident[0:3, 0:1], 0.0, ALU.mult, ALU.add))
            then(nc.gpsimd.tensor_scalar(row_part[:, :], row_mid[:, :], ident[0:3, 1:2], 0.0, ALU.mult, ALU.add))
            then(nc.gpsimd.tensor_tensor(row_pick[:, :], row_pick[:, :], row_part[:, :], ALU.add))
            then(nc.gpsimd.tensor_scalar(row_part[:, :], row_rest[:, :], ident[0:3, 2:3], 0.0, ALU.mult, ALU.add))
            nc.gpsimd.tensor_tensor(bias_rows[0:3, :], row_pick[:, :], row_part[:, :],
                                    ALU.add).then_inc(bias_rows_ready, 1)
            pool.wait_ge(bias_rows_ready, 1)
            for g in range(GROUPS):
                rotate(0, g)
            finish_terms(0)
            scale_twisted(0, 0)
            for g in range(GROUPS):
                if g + 1 < GROUPS:
                    scale_twisted(0, g + 1)
                rstd(GROUPS + g)
            for g in range(GROUPS):
                rstd(2 * GROUPS + g)
            for g in range(GROUPS):
                rotate(1, g)
            finish_terms(1)
            for g in range(GROUPS):
                scale_twisted(1, g)

        @block.scalar
        def _(act):
            act.dma_start(early_sb[:, :], early).then_inc(early_loaded, 16)
            act.dma_start(net_sb[:, :], net).then_inc(net_loaded, 16)
            nc.scalar.preload_act_table_set("gelu_and_others")

            def take_transposed(use, dst, func=ACT.Identity, bias=0.0):
                act.wait_ge(trans_done, use + 1)
                nc.scalar.activation(dst, trans_ps[use % 2][:, :], func, bias=bias).then_inc(trans_read, 1)

            def gelu1(f, s):
                n = ITEMS * f + s
                if n >= 2:
                    act.wait_ge(l2_done, n - 1)
                take_transposed(use_pre(f, s), h1[:, n % 2], ACT.Gelu, vec("b1"))

            def gelu2(f, s):
                n = ITEMS * f + s
                act.wait_ge(l2_done, n + 1)
                if n >= 2:
                    act.wait_ge(l3_done, n - 1)
                nc.scalar.activation(h2[:, n % 2], l2_ps[:, 0:GW // 2], ACT.Gelu,
                                     bias=vec("b2")).then_inc(gelu2_done, 1)

            def gelu3(f, s):
                n = ITEMS * f + s
                act.wait_ge(l3_done, n + 1)
                if n >= 2:
                    act.wait_ge(l4_done, n - 1)
                nc.scalar.activation(h3[:, n % 2], l3_ps[:, 0:GW // 4], ACT.Gelu,
                                     bias=vec("b3")).then_inc(gelu3_done, 1)

            def tanh(f, s):
                n = ITEMS * f + s
                act.wait_ge(l4_done, n + 1)
                nc.scalar.activation(tf[:, n], l4_ps[:, 0:GS], ACT.Tanh, bias=half_b4, scale=0.5
                                     ).then_inc(tanh_done, 1)

            def take_ln(f, g):
                act.wait_ge(trans_done, use_ln(f, g) + 1)
                for b in range(B):
                    src = trans_ps[use_ln(f, g) % 2][:, :].rearrange("p (s b t) -> p b s t", s=GS, b=B)[:, b]
                    dst = lnT[:, GW * g:GW * g + GW].rearrange("p (s b t) -> p b s t", s=GS, b=B)[:, b]
                    last = nc.scalar.activation(dst, src, ACT.Identity, accum_out=token_sum[:, f, g, b:b + 1])
                last.then_inc(trans_read, 1)

            def normalise(n):
                act.wait_ge(rstd_ready, n + 1)
                layer, g = divmod(n, GROUPS)
                act.wait_ge((x_mid_ready, x_att_ready)[layer - 1], g + 1)
                for j in range(GS):
                    last = nc.scalar.activation(ln[:, GS * g + j], LN_SRC[layer][:, GS * g + j], ACT.Identity,
                                                scale=small[:, n, 2, j:j + 1], bias=small[:, n, 3, j:j + 1])
                last.then_inc(ln_ready, 1)

            def twist(f, g):
                src = group(ln, g).rearrange("p s (q e) -> p s q e", q=4)
                dst = group(tln, g).rearrange("p s (q e) -> p s q e", q=4)
                nc.scalar.activation(dst[:, :, 0:4:3], src[:, :, 2:0:-1], ACT.Identity)
                nc.scalar.activation(dst[:, :, 1:3], src[:, :, 3::-3], ACT.Identity,
                                     scale=-1.0).then_inc(tln_ready, 1)

            def context_step(f, k):
                act.wait_ge(gf_pe, 3 * f + k + 1)
                if k == 0:
                    ins = nc.scalar.activation(gf[0:64, f, 2:4], gf_ps[0:64, 8:10], ACT.Gelu, bias=vec("gc1", 64),
                                               scale=1.0 / N)
                elif k == 1:
                    wide = gf_ps[0:32, 16:18].unsqueeze(2).to_broadcast([32, B, T])
                    ins = nc.scalar.activation(g2x[:, f, :].rearrange("p (b t) -> p b t", b=B), wide, ACT.Gelu,
                                               bias=vec("gc2", 32))
                else:
                    ins = nc.scalar.activation(gf[:, f, 6:7], gf_ps[:, 24:25], ACT.Tanh, bias=half_gb3, scale=0.5)
                ins.then_inc(gf_act, 1)

            def ffn(f):
                for g in range(2):
                    if f:
                        normalise(2 * GROUPS + g)
                for g in range(2):
                    take_ln(f, g)
                for k in range(GROUPS):
                    if k >= 1:
                        gelu2(f, k - 1)
                    gelu1(f, k)
                    if k >= 2:
                        tanh(f, k - 2)
                    if k >= 1:
                        gelu3(f, k - 1)
                    if k == 2:
                        context_step(f, 1)
                    if k + 2 < GROUPS:
                        if f:
                            normalise(2 * GROUPS + k + 2)
                        take_ln(f, k + 2)
                    if k in (1, 2):
                        context_step(f, 2 * k - 2)
                gelu1(f, GROUPS)
                for k in range(GROUPS, ITEMS + 2):
                    tanh(f, k - 2)
                    if k < ITEMS + 1:
                        gelu2(f, k - 1)
                    if k + 1 < ITEMS:
                        gelu1(f, k + 1)
                    if k < ITEMS + 1:
                        gelu3(f, k - 1)
                    if GROUPS <= k < 2 * GROUPS:
                        twist(f, k - GROUPS)

            act.wait_ge(early_loaded, 16)
            for dst, src, by in ((half_b4, "b4", 0.5), (half_gb3, "gc3", 0.5), (range_07, "range", 0.7),
                                 (range_03, "range", 0.3)):
                ins = nc.scalar.activation(dst, vec(src), ACT.Identity, scale=by)
            ins.then_inc(consts_ready, 1)
            for p in (0, 96):
                m = early_sb[p:p + 32, EARLY["w1t"][0]:EARLY["w1t"][1]]
                ins = nc.scalar.activation(m, m, ACT.Identity, scale=-1.0)
            ins.then_inc(signs_ready, 1)
            act.wait_ge(consts_ready, 1)
            ffn(0)
            def take_proj1(g, i):
                dst, bias = ((h1q, vec("q1")), (h1k, vec("k1")), (vT, vec("v")), (gate, 0.0))[i]
                act.wait_ge(proj1_done, 4 * g + i + 1)
                if i == 3:
                    d, src = group(dst, g).rearrange("p s e -> p (s e)"), bank[2 + i][:, :]
                else:
                    d = dst[:, :, GS * g:GS * g + GS, :].rearrange("p b s t -> p s b t")
                    src = bank[2 + i][:, :].rearrange("p (s b t) -> p s b t", s=GS, b=B)
                nc.scalar.activation(d, src, ACT.Gelu, bias=bias).then_inc(proj1_read, 1)

            normalise(GROUPS)
            take_transposed(use_ln_att(0), lnT[:, 0:GW])
            for g in range(GROUPS):
                take_proj1(g, 0)
                if g + 1 < GROUPS:
                    normalise(GROUPS + g + 1)
                take_proj1(g, 1)
                take_proj1(g, 2)
                if g + 1 < GROUPS:
                    take_transposed(use_ln_att(g + 1), lnT[:, GW * (g + 1):GW * (g + 2)])
                take_proj1(g, 3)
            nc.scalar.preload_act_table_set("natural_log_exp_and_others")
            for n in range(8 + 2):
                if n < 8:
                    act.wait_ge(qk_done, n + 1)
                    e = qk[:, n].rearrange("p s e -> p (s e)")
                    nc.scalar.activation(e, soft_ps[n % 6][:, :], ACT.Exp).then_inc(exp_done, 1)
                if n >= 2:
                    act.wait_ge(clamp_done, n - 1)
                    e = qk[:, n - 2].rearrange("p s e -> p (s e)")
                    nc.scalar.activation(e, e, ACT.Ln, bias=1.0).then_inc(log_done, 1)
            nc.scalar.preload_act_table_set("gelu_and_others")
            for hg in range(GROUPS):
                take_transposed(use_og(hg), group(ogT, hg).rearrange("p h e -> p (h e)"))
            ffn(1)

        @block.vector
        def _(dve):
            steps = [0]

            def then(ins):
                steps[0] += 1
                ins.then_inc(dve_step, 1)
                dve.wait_ge(dve_step, steps[0])

            def bn_stats(n):
                layer, g = divmod(n, GROUPS)
                if layer == 0:
                    dve.wait_ge(x_loaded[g], 16)
                else:
                    dve.wait_ge((x_mid_ready, x_att_ready)[layer - 1], g + 1)
                for j in range(GS):
                    last = nc.vector.bn_stats(stats[:, n, j], LN_SRC[layer][:, GS * g + j])
                last.then_inc(stats_ready, 1)
                dve.wait_ge(stats_ready, n + 1)
                for j in range(GS):
                    last = nc.vector.bn_aggr(moments[:, n, j], stats[:, n, j])
                last.then_inc(moments_ready, 1)

            def normalise(g):
                dve.wait_ge(rstd_ready, g + 1)
                for j in range(GS):
                    last = nc.vector.tensor_scalar(ln[:, GS * g + j], x_in[:, GS * g + j],
                                                   small[:, g, 2, j:j + 1], small[:, g, 3, j:j + 1],
                                                   ALU.mult, ALU.add)
                last.then_inc(ln_ready, 1)

            def take_pq(f, g):
                for half in range(2):
                    dve.wait_ge(pq_done, 2 * (GROUPS * f + g) + half + 1)
                    at = GS * g + 2 * half
                    nc.vector.tensor_copy(pq[:, at:at + 2].rearrange("p s k e -> p (s k e)"),
                                          pq_ps[half][:, :]).then_inc(pq_read, 1)

            def update(f, s):
                cycle, g = divmod(s, GROUPS)
                dve.wait_ge(tanh_done, ITEMS * f + s - GROUPS + 1)
                nc.vector.tensor_scalar(coef[:, f, C1 + cycle - 1, g], tf[:, ITEMS * f + s - GROUPS], range_03,
                                        alpha[:, f:f + 1], ALU.mult, ALU.add).then_inc(coupling_ready, 1)
                dve.wait_ge(coupling_ready, 2 * GROUPS * f + s - GROUPS + 1)
                if cycle == 2:
                    dve.wait_ge(rot_ready, GROUPS * f + g + 1)
                for j in range(GS):
                    at = GS * g + j
                    if cycle == 1:
                        turn, base = pq[:, at, 1], pq[:, at, 0]
                    else:
                        turn, base = rot[:, at], pre[:, at]
                    nc.vector.scalar_tensor_tensor(
                        pre[:, at], turn, coef[:, f, C1 + cycle - 1, g, j:j + 1], base,
                        ALU.mult, ALU.add).then_inc(pre_ready, 1)

            def finish_coef(f, g):
                dve.wait_ge(tanh_done, ITEMS * f + 2 * GROUPS + g + 1)
                dve.wait_ge(terms_ready, f + 1)
                t = tf[:, ITEMS * f + 2 * GROUPS + g].unsqueeze(1).to_broadcast([128, 2, GS])
                then(nc.vector.tensor_tensor(coef[:, f, PART:PART + 2, g], coef[:, f, DIR:DIR + 2, g], t,
                                             ALU.mult))
                nc.vector.tensor_tensor(coef[:, f, AB3:AB3 + 2, g], coef[:, f, PART:PART + 2, g],
                                        coef[:, f, BASE:BASE + 2, g], ALU.add).then_inc(finish_coef_ready, 1)

            def finish_straight(f, g):
                src, dst = ((x_in, x_mid), (x_att, x_out))[f]
                dve.wait_ge(finish_coef_ready, GROUPS * f + g + 1)
                for j in range(GS):
                    at = GS * g + j
                    last = nc.vector.scalar_tensor_tensor(
                        dst[:, at], ln[:, at], coef[:, f, AB3, g, j:j + 1], src[:, at], ALU.mult, ALU.add)
                last.then_inc(straight_ready, 1)

            def finish_twisted(f, g):
                dst = (x_mid, x_out)[f]
                dve.wait_ge(straight_ready, GROUPS * f + g + 1)
                dve.wait_ge(twisted_ready, GROUPS * f + g + 1)
                nc.vector.tensor_tensor(group(dst, g), group(dst, g), group(tln, g),
                                        ALU.add).then_inc((x_mid_ready, x_out_ready)[f], 1)

            def ffn_cycles(f):
                dve.wait_ge(consts_ready, 1)
                dve.wait_ge(gf_act, 3 * f + 3)
                nc.vector.tensor_scalar(alpha[:, f:f + 1], gf[:, f, 6:7], range_07, BASE_COUPLING,
                                        ALU.mult, ALU.add).then_inc(alpha_ready, 1)
                dve.wait_ge(alpha_ready, f + 1)
                for s in range(GROUPS, ITEMS):
                    update(f, s)
                finish_coef(f, 0)
                finish_straight(f, 0)
                for g in range(GROUPS):
                    if g + 1 < GROUPS:
                        finish_coef(f, g + 1)
                        finish_straight(f, g + 1)
                    finish_twisted(f, g)
                    if f == 0:
                        bn_stats(GROUPS + g)

            bn_stats(0)
            bn_stats(1)
            for g in range(GROUPS):
                normalise(g)
                if g + 2 < GROUPS:
                    bn_stats(g + 2)
                if g == 2:
                    take_pq(0, 0)
            for g in range(1, GROUPS):
                take_pq(0, g)
            ffn_cycles(0)

            def mix_first(b):
                dve.wait_ge(a_done, b + 1)
                nc.vector.tensor_tensor(am[:, b], bank[6 + b][:, 0:D], A("mask"), ALU.mult).then_inc(am_ready, 1)

            def mix_second(b):
                dve.wait_ge(zsum_done, b + 1)
                nc.vector.tensor_scalar(zr[:, b], bank[6 + b][:, D:2 * D], float(D), None, ALU.add)
                dve.wait_ge(am_ready, b + 1)
                then(nc.vector.tensor_tensor(ai[:, b], am[:, b], ident, ALU.add))
                then(nc.vector.reciprocal(zi[:, b], zr[:, b]))
                nc.vector.tensor_tensor(mix[:, b], ai[:, b], zi[:, b], ALU.mult).then_inc(mix_ready, 1)

            dve.wait_ge(att_loaded, 16)
            for n in range(8 + 3):
                if n >= 3:
                    dve.wait_ge(log_done, n - 2)
                    e = qk[:, n - 3].rearrange("p s e -> p (s e)")
                    nc.vector.tensor_tensor(e, e, soft_ps[(n - 3) % 6][:, :], ALU.max).then_inc(soft_done, 1)
                if n < 8:
                    dve.wait_ge(exp_done, n + 1)
                    e = qk[:, n].rearrange("p s e -> p (s e)")
                    nc.vector.tensor_scalar(e, e, EXP_TOP, None, ALU.min).then_inc(clamp_done, 1)
                if n == 8:
                    mix_first(0)
                if n == 9:
                    mix_second(0)
            mix_first(1)
            mix_second(1)
            for g in range(GROUPS):
                dve.wait_ge(mixed_done, g + 1)
                nc.vector.tensor_tensor(og[:, :, GS * g:GS * g + GS, :].rearrange("p h j n -> p j h n"),
                                        bank[2 + g][:, :].rearrange("p (j h n) -> p j h n", j=GS, h=H),
                                        group(gate, g).rearrange("p j (h n) -> p j h n", h=H),
                                        ALU.mult).then_inc(og_ready, 1)
            dve.wait_ge(x_att_loaded, 16 * B)
            for hg in range(GROUPS):
                dve.wait_ge(proj_done, hg + 1)
                r = group(x_att, hg).rearrange("p h e -> p (h e)")
                nc.vector.tensor_tensor(r, bank[2 + hg][:, :], r, ALU.add).then_inc(x_att_ready, 1)
                bn_stats(2 * GROUPS + hg)
            for g in range(GROUPS):
                take_pq(1, g)
            ffn_cycles(1)

        @block.tensor
        def _(pe):
            def keep_warm(free_bank, times):
                for _ in range(times):
                    nc.tensor.matmul(free_bank[:, 0:128], ones_bf[:, :], ones_bf[:, :], start=True, stop=True)

            def transpose_group(use, tiles, first_ready=None):
                if use >= 2:
                    pe.wait_ge(trans_read, use - 1)
                for j, tile in enumerate(tiles):
                    if first_ready is not None:
                        pe.wait_ge(pre_ready, first_ready + j)
                    last = nc.tensor.transpose(trans_ps[use % 2][:, D * j:D * j + D], tile, ident)
                last.then_inc(trans_done, 1)

            def transpose_ln(layer, g, use):
                pe.wait_ge(ln_ready, GROUPS * layer + g + 1)
                transpose_group(use, [ln[:, GS * g + j] for j in range(GS)])

            def products_pq(f, g):
                pe.wait_ge(trans_read, use_ln(f, g) + 1)
                for half in range(2):
                    if f or g:
                        pe.wait_ge(pq_read, 2 * (GROUPS * f + g) + half - 1)
                    for j in range(2):
                        at = D * (GS * g + 2 * half + j)
                        last = nc.tensor.matmul(pq_ps[half][:, 2 * D * j:2 * D * (j + 1)], lnT[:, at:at + D],
                                                early_sb[:, EARLY["w1"][0]:EARLY["w1t"][1]],
                                                start=True, stop=True)
                    last.then_inc(pq_done, 1)

            def transpose_pre(f, s):
                cycle, g = divmod(s, GROUPS)
                if cycle == 0:
                    pe.wait_ge(pq_read, 2 * (GROUPS * f + g) + 2)
                    tiles = [pq[:, GS * g + j, 0] for j in range(GS)]
                    transpose_group(use_pre(f, s), tiles)
                else:
                    tiles = [pre[:, GS * g + j] for j in range(GS)]
                    transpose_group(use_pre(f, s), tiles, first_ready=GS * (2 * GROUPS * f + s - GROUPS) + 1)

            def layer2(f, s):
                n = ITEMS * f + s
                pe.wait_ge(trans_read, use_pre(f, s) + 1)
                if n:
                    pe.wait_ge(gelu2_done, n)
                if n == ITEMS:
                    pe.wait_ge(x_att_ready, 3)
                for half in range(2):
                    last = nc.tensor.matmul(l2_ps[64 * half:64 * half + 64, 0:GW // 2], W("w2"),
                                            h1[:, n % 2, GW // 2 * half:GW // 2 * (half + 1)],
                                            start=True, stop=True)
                last.then_inc(l2_done, 1)

            def layer3(f, s):
                n = ITEMS * f + s
                pe.wait_ge(gelu2_done, n + 1)
                if n:
                    pe.wait_ge(gelu3_done, n)
                if n == ITEMS:
                    pe.wait_ge(x_att_ready, 4)
                for half in range(2):
                    last = nc.tensor.matmul(l3_ps[64 * half:64 * half + 64, 0:D], W("w3"),
                                            h2[:, n % 2, D * half:D * half + D], start=True, stop=True)
                last.then_inc(l3_done, 1)

            def layer4(f, s):
                n = ITEMS * f + s
                pe.wait_ge(gelu3_done, n + 1)
                if n:
                    pe.wait_ge(tanh_done, n)
                nc.tensor.matmul(l4_ps[:, 0:GS], h3[:, n % 2], W("w4"), start=True, stop=True).then_inc(l4_done, 1)

            def context_step(f, k):
                if k == 0:
                    pe.wait_ge(trans_read, use_ln(f, GROUPS - 1) + 1)
                    for g in range(GROUPS):
                        ins = nc.tensor.matmul(gf_ps[0:64, 8:10], W("gc1"), token_sum[:, f, g],
                                               start=(g == 0), stop=(g == GROUPS - 1))
                else:
                    pe.wait_ge(gf_act, 3 * f + k)
                    if k == 1:
                        ins = nc.tensor.matmul(gf_ps[0:32, 16:18], W("gc2", 64), gf[0:64, f, 2:4],
                                               start=True, stop=True)
                    else:
                        ins = nc.tensor.matmul(gf_ps[:, 24:25], g2x[:, f], W("gc3", 32), start=True, stop=True)
                ins.then_inc(gf_pe, 1)

            def ffn(f):
                transpose_ln(2 * f, 0, use_ln(f, 0))
                transpose_ln(2 * f, 1, use_ln(f, 1))
                products_pq(f, 0)
                for k in range(GROUPS):
                    transpose_pre(f, k)
                    if k >= 2:
                        layer4(f, k - 2)
                    if k >= 1:
                        layer3(f, k - 1)
                    if k == 2:
                        context_step(f, 1)
                    if k + 2 < GROUPS:
                        transpose_ln(2 * f, k + 2, use_ln(f, k + 2))
                    if k + 1 < GROUPS:
                        products_pq(f, k + 1)
                    if k in (1, 2):
                        context_step(f, 2 * k - 2)
                    layer2(f, k)
                transpose_pre(f, GROUPS)
                for k in range(GROUPS, ITEMS + 2):
                    layer4(f, k - 2)
                    if k + 1 < ITEMS:
                        transpose_pre(f, k + 1)
                    if k < ITEMS + 1:
                        layer3(f, k - 1)
                    if k < ITEMS:
                        layer2(f, k)

            def biased(dst, row, tiles, weights):
                bias = bias_rows[:, D * ROWS[row]:D * ROWS[row] + D].unsqueeze(1).to_broadcast([128, GS, D])
                nc.tensor.matmul(dst[:, :].rearrange("p (j e) -> p j e", j=GS), ones_bf[:, :], bias,
                                 start=True, stop=False, skip_group_check=True)
                for j, tile in enumerate(tiles):
                    last = nc.tensor.matmul(dst[:, D * j:D * j + D], tile, weights, start=False,
                                            stop=(j == GS - 1), skip_group_check=True)
                return last

            pe.wait_ge(ones_ready, 1)
            keep_warm(gf_ps, 50)
            pe.wait_ge(early_loaded, 16)
            pe.wait_ge(net_loaded, 16)
            pe.wait_ge(signs_ready, 1)
            ffn(0)
            pe.wait_ge(gelu2_done, ITEMS)
            pe.wait_ge(gelu3_done, ITEMS)
            pe.wait_ge(att_loaded, 16)
            pe.wait_ge(bias_rows_ready, 1)
            transpose_ln(1, 0, use_ln_att(0))
            for g in range(GROUPS):
                pe.wait_ge(trans_read, use_ln_att(g) + 1)
                for i, name in enumerate(("q1", "k1", "v")):
                    if g:
                        pe.wait_ge(proj1_read, 4 * (g - 1) + i + 1)
                    nc.tensor.matmul(bank[2 + i][:, :], A(name), lnT[:, GW * g:GW * g + GW],
                                     start=True, stop=True).then_inc(proj1_done, 1)
                if g + 1 < GROUPS:
                    transpose_ln(1, g + 1, use_ln_att(g + 1))
                if g:
                    pe.wait_ge(proj1_read, 4 * g)
                biased(bank[5], "g", [lnT[:, D * (GS * g + j):D * (GS * g + j + 1)] for j in range(GS)],
                       A("g")).then_inc(proj1_done, 1)

            def softplus_inputs(i):
                b, u = divmod(i, 2)
                for x_, (h, row) in enumerate(((h1q, "q2"), (h1k, "k2"))):
                    n = 2 * i + x_
                    if i == 2:
                        pe.wait_ge(trans_read, use_ln_att(GROUPS - 1) + 1)
                    elif i < 2:
                        pe.wait_ge(proj1_read, 4 * (GROUPS - 1) + n + 1)
                    else:
                        pe.wait_ge(soft_done, n - 5)
                    tiles = [h[:, b, 8 * u + 2 * j:8 * u + 2 * j + 2, :].rearrange("p s t -> p (s t)")
                             for j in range(GS)]
                    biased(soft_ps[n % 6], row, tiles, A(row)).then_inc(qk_done, 1)

            def product_qk(i):
                b, u = divmod(i, 2)
                pe.wait_ge(soft_done, 2 * i + 2)
                if i == 0:
                    pe.wait_ge(tanh_done, ITEMS)
                for j in range(GS):
                    last = nc.tensor.matmul(bank[6 + b][:, 0:D], qk[:, 2 * i + 1, j], qk[:, 2 * i, j],
                                            start=(u == 0 and j == 0), stop=(u == 1 and j == GS - 1))
                if u == 1:
                    last.then_inc(a_done, 1)

            def z_sum(b):
                pe.wait_ge(am_ready, b + 1)
                nc.tensor.matmul(bank[6 + b][:, D:2 * D], A("ones"), am[:, b], start=True,
                                 stop=True).then_inc(zsum_done, 1)

            softplus_inputs(0)
            softplus_inputs(1)
            softplus_inputs(2)
            product_qk(0)
            softplus_inputs(3)
            product_qk(1)
            z_sum(0)
            product_qk(2)
            product_qk(3)
            z_sum(1)
            for g in range(GROUPS):
                pe.wait_ge(soft_done, 8)
                pe.wait_ge(mix_ready, B)
                for j in range(GS):
                    for b in range(B):
                        last = nc.tensor.matmul(bank[2 + g][T * b:T * b + T, D * j:D * j + D],
                                                vT[:, b, GS * g + j, :], mix[:, b], start=True, stop=True)
                last.then_inc(mixed_done, 1)
            pe.wait_ge(og_ready, GROUPS)
            def transpose_og(hg):
                transpose_group(use_og(hg), [og[:, GS * hg + j].rearrange("p j n -> p (j n)") for j in range(GS)])

            transpose_og(0)
            for hg in range(GROUPS):
                if hg + 1 < GROUPS:
                    transpose_og(hg + 1)
                pe.wait_ge(trans_read, use_og(hg) + 1)
                biased(bank[2 + hg], "p", [ogT[:, GS * hg + j] for j in range(GS)], A("p")).then_inc(proj_done, 1)
            pe.wait_ge(x_att_ready, 2)
            ffn(1)


def kernel(**inputs):
    import numpy as np
    import concourse.bacc as bacc
    from concourse import mybir as mb
    from concourse.bass_utils import run_bass_kernel_spmd

    a = {k.replace("L0_", "", 1): np.asarray(v) for k, v in inputs.items()}
    early = np.zeros((128, width(EARLY)), np.float32)
    net = np.zeros((128, width(NET)), np.float32)
    att = np.zeros((128, width(ATT)), np.float32)

    def put(dst, table, name, value, row=0, col=0):
        c = table[name][0] + col
        dst[row:row + value.shape[0], c:c + value.shape[1]] = value

    put(early, EARLY, "ident", np.eye(128, dtype=np.float32))
    w1 = a["ffn_cn_w1"]
    put(early, EARLY, "w1", w1)
    put(early, EARLY, "w1t", np.concatenate([w1[64:96], w1[96:128], w1[0:32], w1[32:64]]))
    for b in range(B):
        early[T * b:T * b + T, EARLY["sel"][0] + b] = 1.0 / N
    columns = dict(b1=(a["ffn_cn_b1"], 1), b2=(a["ffn_cn_b2"], 2), b3=(a["ffn_cn_b3"], 4),
                   q1=(a["attn_q_b1"], 1), k1=(a["attn_k_b1"], 1), v=(a["attn_v_b"], 1), b4=(a["ffn_cn_b4"], 128),
                   gc1=(a["ffn_gc_b1"], 1), gc2=(a["ffn_gc_b2"], 1), gc3=(a["ffn_gc_b3"], 128),
                   range=(a["ffn_adaptive_range"], 128))
    for name, (value, times) in columns.items():
        v = np.tile(value, times)
        early[0:v.shape[0], EARLY["vec"][0] + VEC[name]] = v
    put(net, NET, "w2", a["ffn_cn_w2"])
    for i in range(2):
        put(net, NET, "w3", a["ffn_cn_w3"], 64 * i, 32 * i)
    for i, slot in enumerate((0, 2, 1, 3)):
        put(net, NET, "w4", a["ffn_cn_w4"], 32 * i, slot)
    for i in (1, 2, 3):
        put(net, NET, f"gc{i}", a[f"ffn_gc_w{i}"])
    for name, key in dict(q1="q_w1", k1="k_w1", v="v_w", g="g_w", q2="q_w2", k2="k_w2", p="p_w").items():
        put(att, ATT, name, a["attn_" + key].T)
    put(att, ATT, "mask", np.kron(np.eye(H), np.full((HD, HD), SCALE)).astype(np.float32))
    put(att, ATT, "ones", np.ones((128, 128), np.float32))
    rows = np.tile(np.concatenate([a["attn_g_b"], a["attn_q_b2"], a["attn_k_b2"], a["attn_p_b"]])[None], (3, 1))
    arrays = dict(x=np.ascontiguousarray(a["attn_x"].reshape(B * N, D)), early=early, net=net, att=att,
                  rows=np.ascontiguousarray(rows))

    nc = bacc.Bacc("TRN2", target_bir_lowering=False, num_devices=1)
    args = [nc.dram_tensor(f"in_{k}", v.shape, mb.dt.from_np(v.dtype), kind="ExternalInput").ap()
            for k, v in arrays.items()]
    out = nc.dram_tensor("out_x", (B * N, D), mb.dt.float32, kind="ExternalOutput").ap()
    build(nc, *args, out)
    r = run_bass_kernel_spmd(nc, [{f"in_{k}": v for k, v in arrays.items()}], core_ids=[0])
    return r.results[0]["out_x"].reshape(B, N, D)
```

```python
import concourse.bass as bass
import concourse.mybir as mybir
from concourse.alu_op_type import AluOpType as ALU
from contextlib import ExitStack

B, N, D, H = 2, 1024, 128, 16
HD = D // H
SLOTS = B * N // D
T = N // SLOTS
GROUPS, GS = 4, SLOTS // 4
GW = GS * D
CYCLES = 3
ITEMS = CYCLES * GROUPS
SCALE = HD ** -0.5
EPS = 1e-5
EXP_TOP = 2.0 ** 60
BASE_COUPLING = 0.1

EARLY = dict(ident=(0, 128), w1=(128, 256), w1t=(256, 384), vec=(384, 400))
NET = dict(w2=(0, 64), w3=(64, 128), w4=(128, 132), gc1=(132, 196), gc2=(196, 228), gc3=(228, 229))
ATT = dict(q1=(0, 128), k1=(128, 256), v=(256, 384), g=(384, 512), q2=(512, 640), k2=(640, 768),
           p=(768, 896), mask=(896, 1024), ones=(1024, 1152))
C1, C2, PROD, SUM, AB2, TURN2, BASE, DIR, PART, AB3 = 0, 1, 2, 3, 4, 6, 8, 10, 12, 14
VEC = dict(b1=0, b2=1, b3=2, q1=3, k1=4, v=5, b4=6, gc1=7, gc2=8, gc3=9, range=10)
ROWS = dict(g=0, q2=1, k2=2, p=3)


def width(table):
    return max(end for _, end in table.values())


def build(nc, x, early, net, att, rows, out):
    f32, bf16 = mybir.dt.float32, mybir.dt.bfloat16
    ACT = mybir.ActivationFunctionType
    scratch = nc.dram_tensor("x_mid_scratch", (B * N, D), f32).ap()

    with ExitStack() as ctx:
        def sb(name, shape, dt=f32):
            return ctx.enter_context(nc.sbuf_tensor(name, shape, dt))

        def sem(name):
            return ctx.enter_context(nc.semaphore(name))

        early_sb = sb("early_sb", [128, width(EARLY)])
        net_sb = sb("net_sb", [128, width(NET)])
        att_sb = sb("att_sb", [128, width(ATT)])
        rows_sb = sb("rows_sb", [3, 4 * D])

        def E(name):
            return early_sb[:, EARLY[name][0]:EARLY[name][1]]

        def W(name, parts=128):
            return net_sb[0:parts, NET[name][0]:NET[name][1]]

        def A(name):
            return att_sb[:, ATT[name][0]:ATT[name][1]]

        def vec(name, parts=128):
            at = EARLY["vec"][0] + VEC[name]
            return early_sb[0:parts, at:at + 1]

        ident = E("ident")
        derived = sb("derived", [128, 4])
        half_b4, half_gb3, range_07, range_03 = (derived[:, i:i + 1] for i in range(4))
        minus_half = sb("minus_half", [128, GS])
        ones_bf = sb("ones_bf", [128, 128], bf16)
        row_rest = sb("row_rest", [3, 4 * D])
        row_hi = sb("row_hi", [3, 4 * D], bf16)
        row_mid = sb("row_mid", [3, 4 * D], bf16)
        row_lo = sb("row_lo", [3, 4 * D], bf16)
        row_pick = sb("row_pick", [3, 4 * D])
        row_part = sb("row_part", [3, 4 * D])
        bias_rows = sb("bias_rows", [128, 4 * D], bf16)

        x_in = sb("x_in", [128, SLOTS, D])
        x_mid = sb("x_mid", [128, SLOTS, D])
        x_att = sb("x_att", [128, SLOTS, D])
        x_out = sb("x_out", [128, SLOTS, D])
        ln = sb("ln", [128, SLOTS, D])
        tln = sb("tln", [128, SLOTS, D])
        lnT = sb("lnT", [128, SLOTS * D])
        pq = sb("pq", [128, SLOTS, 2, D])
        pre = sb("pre", [128, SLOTS, D])
        rot = sb("rot", [128, SLOTS, D])
        token_sum = sb("token_sum", [128, 2, GROUPS, B])
        stats = sb("stats", [128, 3 * GROUPS, GS, 6])
        moments = sb("moments", [128, 3 * GROUPS, GS, 2])
        small = sb("small", [128, 3 * GROUPS, 4, GS])
        h1 = sb("h1", [128, 2, GW])
        h2 = sb("h2", [128, 2, GW // 2])
        h3 = sb("h3", [128, 2, GW // 4])
        tf = sb("tf", [128, 2 * ITEMS, GS])
        coef = sb("coef", [128, 2, 16, GROUPS, GS])
        gf = sb("gf", [128, 2, 8])
        g2x = sb("g2x", [32, 2, 128])
        alpha = sb("alpha", [128, 2])
        h1q = sb("h1q", [128, B, SLOTS, T])
        h1k = sb("h1k", [128, B, SLOTS, T])
        vT = sb("vT", [128, B, SLOTS, T])
        gate = sb("gate", [128, SLOTS, D])
        qk = sb("qk", [128, 8, GS, D])
        am = sb("am", [128, B, D])
        ai = sb("ai", [128, B, D])
        zi = sb("zi", [128, B, D])
        mix = sb("mix", [128, B, D])
        og = sb("og", [128, H, SLOTS, HD])
        ogT = sb("ogT", [128, H, D])

        bank = [ctx.enter_context(nc.psum_tensor(f"bank{i}", [128, 512], f32)) for i in range(8)]
        trans_ps = bank[0:2]
        pq_ps = bank[2:4]
        l2_ps, l3_ps, l4_ps, gf_ps = bank[4:8]
        soft_ps = bank[2:6] + bank[0:2]

        x_loaded = [sem(f"x_loaded{g}") for g in range(GROUPS)]
        early_loaded, net_loaded, att_loaded, rows_loaded = (
            sem(n) for n in ("early_loaded", "net_loaded", "att_loaded", "rows_loaded"))
        x_mid_stored, x_att_loaded, out_stored = (sem(n) for n in ("x_mid_stored", "x_att_loaded", "out_stored"))
        ones_ready, consts_ready, signs_ready, bias_rows_ready, pool_step, dve_step = (
            sem(n) for n in ("ones_ready", "consts_ready", "signs_ready", "bias_rows_ready", "pool_step", "dve_step"))
        alpha_ready, terms_ready, straight_ready, ln_first_ready = (
            sem(n) for n in ("alpha_ready", "terms_ready", "straight_ready", "ln_first_ready"))
        eps_added = sem("eps_added")
        part_ready, last_twisted_ready, p_bias_done, p_bias_added = (
            sem(n) for n in ("part_ready", "last_twisted_ready", "p_bias_done", "p_bias_added"))
        stats_ready, moments_ready, rstd_ready, ln_ready, tln_ready = (
            sem(n) for n in ("stats_ready", "moments_ready", "rstd_ready", "ln_ready", "tln_ready"))
        trans_done, trans_read, pq_done, pq_read = (
            sem(n) for n in ("trans_done", "trans_read", "pq_done", "pq_read"))
        coupling_ready, rot_ready, finish_coef_ready, twisted_ready = (
            sem(n) for n in ("coupling_ready", "rot_ready", "finish_coef_ready", "twisted_ready"))
        pre_ready, l2_done, gelu2_done, l3_done, gelu3_done, l4_done, tanh_done = (
            sem(n) for n in ("pre_ready", "l2_done", "gelu2_done", "l3_done", "gelu3_done", "l4_done", "tanh_done"))
        gf_pe, gf_act, x_mid_ready, x_out_ready = (sem(n) for n in ("gf_pe", "gf_act", "x_mid_ready", "x_out_ready"))
        proj1_done, proj1_read, qk_done, exp_done, clamp_done, log_done, soft_done = (
            sem(n) for n in ("proj1_done", "proj1_read", "qk_done", "exp_done", "clamp_done", "log_done",
                             "soft_done"))
        a_done, am_ready, zsum_done, mix_ready, mixed_done, og_ready, proj_done, x_att_ready = (
            sem(n) for n in ("a_done", "am_ready", "zsum_done", "mix_ready", "mixed_done", "og_ready",
                             "proj_done", "x_att_ready"))

        def use_ln(f, g):
            return 24 * f + (0, 1, 3, 5)[g]

        def use_pre(f, s):
            return 24 * f + ((2, 4, 6, 7)[s] if s < GROUPS else GROUPS + s)

        def use_ln_att(g):
            return 16 + g

        def use_og(hg):
            return 20 + hg

        LN_SRC = [x_in, x_mid, x_att]

        def group(t, g):
            return t[:, GS * g:GS * g + GS]

        block = ctx.enter_context(nc.Block())

        def out_group(queue, g, b):
            queue.wait_ge(x_out_ready, g + 1)
            dst = out[N * b + GS * T * g:N * b + GS * T * (g + 1), :].rearrange("(h t) f -> t h f", t=T)
            queue.dma_start(dst, x_out[T * b:T * b + T, GS * g:GS * g + GS, :]).then_inc(out_stored, 16)

        @block.sync
        def _(sp):
            x_v = x.rearrange("(p s) f -> p s f", p=128)
            for g in range(GROUPS):
                sp.dma_start(group(x_in, g), x_v[:, GS * g:GS * g + GS, :]).then_inc(x_loaded[g], 16)
            sp.dma_start(rows_sb[:, :], rows).then_inc(rows_loaded, 16)
            sp.dma_start(att_sb[:, :], att).then_inc(att_loaded, 16)
            s_v = scratch.rearrange("(p s) f -> p s f", p=128)
            for g in range(GROUPS):
                sp.wait_ge(x_mid_ready, g + 1)
                sp.dma_start(s_v[:, GS * g:GS * g + GS, :], group(x_mid, g)).then_inc(x_mid_stored, 16)
            sp.wait_ge(x_mid_stored, 16 * GROUPS)
            for b in range(B):
                sp.dma_start(x_att[T * b:T * b + T, :, :],
                             scratch[N * b:N * b + N, :].rearrange("(h t) f -> t h f", t=T)
                             ).then_inc(x_att_loaded, 16)
            for g in range(GROUPS):
                for b in range(B):
                    if (g, b) != (GROUPS - 1, 1):
                        out_group(sp, g, b)
            sp.wait_ge(out_stored, 16 * GROUPS * B)

        @block.gpsimd
        def _(pool):
            steps = [0]

            def then(ins):
                steps[0] += 1
                ins.then_inc(pool_step, 1)
                pool.wait_ge(pool_step, steps[0])

            def rstd(n):
                mv, o = moments[:, n], small[:, n]
                pool.wait_ge(moments_ready, n + 1)
                nc.gpsimd.tensor_scalar(o[:, 1], mv[:, :, 1], 1.0, EPS, ALU.mult, ALU.add).then_inc(eps_added, 1)
                nc.gpsimd.tensor_scalar(o[:, 0], mv[:, :, 0], -1.0, 0.0, ALU.mult, ALU.add)
                pool.wait_ge(eps_added, n + 1)
                then(nc.gpsimd.tensor_tensor(o[:, 2], o[:, 1], minus_half[:, :], ALU.pow))
                nc.gpsimd.tensor_tensor(o[:, 3], o[:, 2], o[:, 0], ALU.mult).then_inc(rstd_ready, 1)

            def rotate(f, g):
                pool.wait_ge(coupling_ready, 2 * GROUPS * f + g + 1)
                for j in range(GS):
                    at = GS * g + j
                    last = nc.gpsimd.tensor_scalar(rot[:, at], pq[:, at, 0], coef[:, f, C1, g, j:j + 1],
                                                   -1.0, ALU.mult, ALU.mult)
                then(last)
                nc.gpsimd.tensor_tensor(group(rot, g), group(rot, g), group(pq, g)[:, :, 1],
                                        ALU.add).then_inc(rot_ready, 1)

            def finish_terms(f, h):
                def rows(first, count=1):
                    return coef[:, f, first:first + count, 2 * h:2 * h + 2].rearrange("p r g j -> p r (g j)")

                pool.wait_ge(coupling_ready, 2 * GROUPS * f + GROUPS + 2 * h + 2)
                pool.wait_ge(alpha_ready, f + 1)
                nc.gpsimd.tensor_tensor(rows(PROD), rows(C1), rows(C2), ALU.mult)
                then(nc.gpsimd.tensor_tensor(rows(SUM), rows(C1), rows(C2), ALU.add))
                for row, src, by, plus in ((AB2, PROD, -0.5, 0.5), (AB2 + 1, SUM, 0.5, 0.0),
                                           (TURN2, SUM, -0.5, 0.0), (TURN2 + 1, PROD, -0.5, 0.5)):
                    last = nc.gpsimd.tensor_scalar(rows(row), rows(src), by, plus, ALU.mult, ALU.add)
                then(last)
                nc.gpsimd.tensor_scalar(rows(DIR, 2), rows(TURN2, 2), range_03, 0.0, ALU.mult, ALU.add)
                then(nc.gpsimd.tensor_scalar(rows(BASE, 2), rows(TURN2, 2), alpha[:, f:f + 1], 0.0,
                                             ALU.mult, ALU.add))
                nc.gpsimd.tensor_tensor(rows(BASE, 2), rows(BASE, 2), rows(AB2, 2),
                                        ALU.add).then_inc(terms_ready, 1)

            def scale_twisted(f, g):
                pool.wait_ge(tln_ready, GROUPS * f + g + 1)
                pool.wait_ge(finish_coef_ready, GROUPS * f + g + 1)
                for j in range(GS if f else GS // 2):
                    t = tln[:, GS * g + j]
                    last = nc.gpsimd.tensor_scalar(t, t, coef[:, f, AB3 + 1, g, j:j + 1], 0.0,
                                                   ALU.mult, ALU.add)
                last.then_inc(twisted_ready, 1)

            nc.gpsimd.memset(minus_half[:, :], -0.5)
            nc.gpsimd.memset(ones_bf[:, :], 1.0).then_inc(ones_ready, 1)
            then(nc.gpsimd.memset(bias_rows[:, :], 0.0))
            for g in range(GROUPS):
                rstd(g)
            pool.wait_ge(rows_loaded, 16)
            pool.wait_ge(early_loaded, 16)
            then(nc.gpsimd.tensor_copy(row_hi[:, :], rows_sb[:, :]))
            then(nc.gpsimd.tensor_tensor(row_rest[:, :], rows_sb[:, :], row_hi[:, :], ALU.subtract))
            then(nc.gpsimd.tensor_copy(row_mid[:, :], row_rest[:, :]))
            then(nc.gpsimd.tensor_tensor(row_rest[:, :], row_rest[:, :], row_mid[:, :], ALU.subtract))
            then(nc.gpsimd.tensor_scalar(row_pick[:, :], row_hi[:, :], ident[0:3, 0:1], 0.0, ALU.mult, ALU.add))
            then(nc.gpsimd.tensor_scalar(row_part[:, :], row_mid[:, :], ident[0:3, 1:2], 0.0, ALU.mult, ALU.add))
            then(nc.gpsimd.tensor_tensor(row_pick[:, :], row_pick[:, :], row_part[:, :], ALU.add))
            then(nc.gpsimd.tensor_scalar(row_part[:, :], row_rest[:, :], ident[0:3, 2:3], 0.0, ALU.mult, ALU.add))
            nc.gpsimd.tensor_tensor(bias_rows[0:3, :], row_pick[:, :], row_part[:, :],
                                    ALU.add).then_inc(bias_rows_ready, 1)
            pool.wait_ge(bias_rows_ready, 1)
            for g in range(GROUPS):
                rotate(0, g)
            finish_terms(0, 0)
            scale_twisted(0, 0)
            finish_terms(0, 1)
            rstd(GROUPS)
            scale_twisted(0, 1)
            for g in range(1, GROUPS):
                if g + 1 < GROUPS:
                    scale_twisted(0, g + 1)
                rstd(GROUPS + g)
            for g in range(GROUPS):
                rstd(2 * GROUPS + g)
            for g in range(GROUPS):
                rotate(1, g)
            finish_terms(1, 0)
            finish_terms(1, 1)
            for g in range(GROUPS - 1):
                scale_twisted(1, g)

        @block.scalar
        def _(act):
            act.dma_start(early_sb[:, :], early).then_inc(early_loaded, 16)
            act.dma_start(net_sb[:, :], net).then_inc(net_loaded, 16)
            nc.scalar.preload_act_table_set("gelu_and_others")

            def take_transposed(use, dst, func=ACT.Identity, bias=0.0):
                act.wait_ge(trans_done, use + 1)
                nc.scalar.activation(dst, trans_ps[use % 2][:, :], func, bias=bias).then_inc(trans_read, 1)

            def gelu1(f, s):
                n = ITEMS * f + s
                if n >= 2:
                    act.wait_ge(l2_done, n - 1)
                take_transposed(use_pre(f, s), h1[:, n % 2], ACT.Gelu, vec("b1"))

            def gelu2(f, s):
                n = ITEMS * f + s
                act.wait_ge(l2_done, n + 1)
                if n >= 2:
                    act.wait_ge(l3_done, n - 1)
                nc.scalar.activation(h2[:, n % 2], l2_ps[:, 0:GW // 2], ACT.Gelu,
                                     bias=vec("b2")).then_inc(gelu2_done, 1)

            def gelu3(f, s):
                n = ITEMS * f + s
                act.wait_ge(l3_done, n + 1)
                if n >= 2:
                    act.wait_ge(l4_done, n - 1)
                nc.scalar.activation(h3[:, n % 2], l3_ps[:, 0:GW // 4], ACT.Gelu,
                                     bias=vec("b3")).then_inc(gelu3_done, 1)

            def tanh(f, s):
                n = ITEMS * f + s
                act.wait_ge(l4_done, n + 1)
                nc.scalar.activation(tf[:, n], l4_ps[:, 0:GS], ACT.Tanh, bias=half_b4, scale=0.5
                                     ).then_inc(tanh_done, 1)

            def take_ln(f, g):
                act.wait_ge(trans_done, use_ln(f, g) + 1)
                for b in range(B):
                    src = trans_ps[use_ln(f, g) % 2][:, :].rearrange("p (s b t) -> p b s t", s=GS, b=B)[:, b]
                    dst = lnT[:, GW * g:GW * g + GW].rearrange("p (s b t) -> p b s t", s=GS, b=B)[:, b]
                    last = nc.scalar.activation(dst, src, ACT.Identity, accum_out=token_sum[:, f, g, b:b + 1])
                last.then_inc(trans_read, 1)

            def normalise(n):
                act.wait_ge(rstd_ready, n + 1)
                layer, g = divmod(n, GROUPS)
                act.wait_ge((x_mid_ready, x_att_ready)[layer - 1], g + 1)
                for j in range(GS // 2):
                    last = nc.scalar.activation(ln[:, GS * g + j], LN_SRC[layer][:, GS * g + j], ACT.Identity,
                                                scale=small[:, n, 2, j:j + 1], bias=small[:, n, 3, j:j + 1])
                last.then_inc(ln_first_ready, 1)

            def take_pq_first():
                for half in range(2):
                    act.wait_ge(pq_done, 2 * GROUPS + half + 1)
                    nc.scalar.activation(pq[:, 2 * half:2 * half + 2].rearrange("p s k e -> p (s k e)"),
                                         pq_ps[half][:, :], ACT.Identity).then_inc(pq_read, 1)

            def twist(f, g):
                src = group(ln, g).rearrange("p s (q e) -> p s q e", q=4)
                dst = group(tln, g).rearrange("p s (q e) -> p s q e", q=4)
                nc.scalar.activation(dst[:, :, 0:4:3], src[:, :, 2:0:-1], ACT.Identity)
                nc.scalar.activation(dst[:, :, 1:3], src[:, :, 3::-3], ACT.Identity,
                                     scale=-1.0).then_inc(tln_ready, 1)

            def context_step(f, k):
                act.wait_ge(gf_pe, 3 * f + k + 1)
                if k == 0:
                    ins = nc.scalar.activation(gf[0:64, f, 2:4], gf_ps[0:64, 8:10], ACT.Gelu, bias=vec("gc1", 64),
                                               scale=1.0 / N)
                elif k == 1:
                    wide = gf_ps[0:32, 16:18].unsqueeze(2).to_broadcast([32, B, T])
                    ins = nc.scalar.activation(g2x[:, f, :].rearrange("p (b t) -> p b t", b=B), wide, ACT.Gelu,
                                               bias=vec("gc2", 32))
                else:
                    ins = nc.scalar.activation(gf[:, f, 6:7], gf_ps[:, 24:25], ACT.Tanh, bias=half_gb3, scale=0.5)
                ins.then_inc(gf_act, 1)

            def scale_twisted():
                act.wait_ge(finish_coef_ready, 2 * GROUPS)
                for j in range(GS):
                    t = tln[:, GS * (GROUPS - 1) + j]
                    last = nc.scalar.activation(t, t, ACT.Identity, scale=coef[:, 1, AB3 + 1, GROUPS - 1, j:j + 1])
                last.then_inc(last_twisted_ready, 1)

            def ffn(f):
                if f:
                    normalise(2 * GROUPS)
                    normalise(2 * GROUPS + 1)
                take_ln(f, 0)
                if f:
                    normalise(2 * GROUPS + 2)
                    take_pq_first()
                take_ln(f, 1)
                if f:
                    normalise(2 * GROUPS + 3)
                for k in range(GROUPS):
                    if k >= 1:
                        gelu2(f, k - 1)
                    if k in (2, 3):
                        context_step(f, 2 * (k - 2))
                    gelu1(f, k)
                    if k >= 2:
                        tanh(f, k - 2)
                    if k == 2:
                        context_step(f, 1)
                    if k >= 1:
                        gelu3(f, k - 1)
                    if k + 2 < GROUPS:
                        take_ln(f, k + 2)
                    twist(f, k)
                for k in range(GROUPS, ITEMS + 2):
                    if k < ITEMS + 1:
                        gelu2(f, k - 1)
                    tanh(f, k - 2)
                    if k < ITEMS:
                        gelu1(f, k)
                    if k < ITEMS + 1:
                        gelu3(f, k - 1)

            act.wait_ge(early_loaded, 16)
            for dst, src, by in ((half_b4, "b4", 0.5), (half_gb3, "gc3", 0.5), (range_07, "range", 0.7),
                                 (range_03, "range", 0.3)):
                ins = nc.scalar.activation(dst, vec(src), ACT.Identity, scale=by)
            ins.then_inc(consts_ready, 1)
            for p in (0, 96):
                m = early_sb[p:p + 32, EARLY["w1t"][0]:EARLY["w1t"][1]]
                ins = nc.scalar.activation(m, m, ACT.Identity, scale=-1.0)
            ins.then_inc(signs_ready, 1)
            act.wait_ge(consts_ready, 1)
            ffn(0)
            def take_proj1(g, i):
                dst, bias = ((h1q, vec("q1")), (h1k, vec("k1")), (vT, vec("v")), (gate, 0.0))[i]
                act.wait_ge(proj1_done, 4 * g + i + 1)
                if i == 3:
                    d, src = group(dst, g).rearrange("p s e -> p (s e)"), bank[2 + i][:, :]
                else:
                    d = dst[:, :, GS * g:GS * g + GS, :].rearrange("p b s t -> p s b t")
                    src = bank[2 + i][:, :].rearrange("p (s b t) -> p s b t", s=GS, b=B)
                nc.scalar.activation(d, src, ACT.Gelu, bias=bias).then_inc(proj1_read, 1)

            normalise(GROUPS)
            take_transposed(use_ln_att(0), lnT[:, 0:GW])
            for g in range(GROUPS):
                take_proj1(g, 0)
                if g + 1 < GROUPS:
                    normalise(GROUPS + g + 1)
                take_proj1(g, 1)
                if g + 1 < GROUPS:
                    take_proj1(g, 2)
                    take_transposed(use_ln_att(g + 1), lnT[:, GW * (g + 1):GW * (g + 2)])
                    take_proj1(g, 3)
            nc.scalar.preload_act_table_set("natural_log_exp_and_others")
            for n in range(8 + 2):
                if n < 8:
                    act.wait_ge(qk_done, n + 1)
                    e = qk[:, n].rearrange("p s e -> p (s e)")
                    nc.scalar.activation(e, soft_ps[n % 6][:, :], ACT.Exp).then_inc(exp_done, 1)
                if n >= 2:
                    act.wait_ge(clamp_done, n - 1)
                    e = qk[:, n - 2].rearrange("p s e -> p (s e)")
                    nc.scalar.activation(e, e, ACT.Ln, bias=1.0).then_inc(log_done, 1)
            nc.scalar.preload_act_table_set("gelu_and_others")
            take_proj1(GROUPS - 1, 2)
            take_proj1(GROUPS - 1, 3)
            for hg in range(GROUPS):
                take_transposed(use_og(hg), group(ogT, hg).rearrange("p h e -> p (h e)"))
            ffn(1)
            scale_twisted()
            out_group(act, GROUPS - 1, 1)

        @block.vector
        def _(dve):
            steps = [0]

            def then(ins):
                steps[0] += 1
                ins.then_inc(dve_step, 1)
                dve.wait_ge(dve_step, steps[0])

            def bn_stats(n):
                layer, g = divmod(n, GROUPS)
                if layer == 0:
                    dve.wait_ge(x_loaded[g], 16)
                else:
                    dve.wait_ge((x_mid_ready, x_att_ready)[layer - 1], g + 1)
                for j in range(GS):
                    last = nc.vector.bn_stats(stats[:, n, j], LN_SRC[layer][:, GS * g + j])
                last.then_inc(stats_ready, 1)

            def bn_moments(n):
                dve.wait_ge(stats_ready, n + 1)
                for j in range(GS):
                    last = nc.vector.bn_aggr(moments[:, n, j], stats[:, n, j])
                last.then_inc(moments_ready, 1)

            def normalise(n):
                dve.wait_ge(rstd_ready, n + 1)
                layer, g = divmod(n, GROUPS)
                for j in range(GS // 2 if layer else 0, GS):
                    last = nc.vector.tensor_scalar(ln[:, GS * g + j], LN_SRC[layer][:, GS * g + j],
                                                   small[:, n, 2, j:j + 1], small[:, n, 3, j:j + 1],
                                                   ALU.mult, ALU.add)
                last.then_inc(ln_ready, 1)

            def take_pq(f, g):
                for half in range(2):
                    dve.wait_ge(pq_done, 2 * (GROUPS * f + g) + half + 1)
                    at = GS * g + 2 * half
                    nc.vector.tensor_copy(pq[:, at:at + 2].rearrange("p s k e -> p (s k e)"),
                                          pq_ps[half][:, :]).then_inc(pq_read, 1)

            def update(f, s):
                cycle, g = divmod(s, GROUPS)
                dve.wait_ge(tanh_done, ITEMS * f + s - GROUPS + 1)
                nc.vector.tensor_scalar(coef[:, f, C1 + cycle - 1, g], tf[:, ITEMS * f + s - GROUPS], range_03,
                                        alpha[:, f:f + 1], ALU.mult, ALU.add).then_inc(coupling_ready, 1)
                dve.wait_ge(coupling_ready, 2 * GROUPS * f + s - GROUPS + 1)
                if cycle == 2:
                    dve.wait_ge(rot_ready, GROUPS * f + g + 1)
                for j in range(GS):
                    at = GS * g + j
                    if cycle == 1:
                        turn, base = pq[:, at, 1], pq[:, at, 0]
                    else:
                        turn, base = rot[:, at], pre[:, at]
                    nc.vector.scalar_tensor_tensor(
                        pre[:, at], turn, coef[:, f, C1 + cycle - 1, g, j:j + 1], base,
                        ALU.mult, ALU.add).then_inc(pre_ready, 1)

            def finish_part(f, g):
                dve.wait_ge(tanh_done, ITEMS * f + 2 * GROUPS + g + 1)
                dve.wait_ge(terms_ready, 2 * f + g // 2 + 1)
                t = tf[:, ITEMS * f + 2 * GROUPS + g].unsqueeze(1).to_broadcast([128, 2, GS])
                nc.vector.tensor_tensor(coef[:, f, PART:PART + 2, g], coef[:, f, DIR:DIR + 2, g], t,
                                        ALU.mult).then_inc(part_ready, 1)

            def finish_coef(f, g):
                dve.wait_ge(part_ready, GROUPS * f + g + 1)
                nc.vector.tensor_tensor(coef[:, f, AB3:AB3 + 2, g], coef[:, f, PART:PART + 2, g],
                                        coef[:, f, BASE:BASE + 2, g], ALU.add).then_inc(finish_coef_ready, 1)

            def finish_straight(f, g):
                src, dst = ((x_in, x_mid), (x_att, x_out))[f]
                dve.wait_ge(finish_coef_ready, GROUPS * f + g + 1)
                for j in range(GS):
                    at = GS * g + j
                    last = nc.vector.scalar_tensor_tensor(
                        dst[:, at], ln[:, at], coef[:, f, AB3, g, j:j + 1], src[:, at], ALU.mult, ALU.add)
                last.then_inc(straight_ready, 1)

            def finish_twisted(f, g):
                dst = (x_mid, x_out)[f]
                dve.wait_ge(straight_ready, GROUPS * f + g + 1)
                if f == 0:
                    for at in (GS * g + 2, GS * g + 3):
                        nc.vector.scalar_tensor_tensor(
                            dst[:, at], tln[:, at], coef[:, f, AB3 + 1, g, at % GS:at % GS + 1], dst[:, at],
                            ALU.mult, ALU.add)
                    if g >= 1:
                        normalise(GROUPS + g - 1)
                if f and g == GROUPS - 1:
                    dve.wait_ge(last_twisted_ready, 1)
                else:
                    dve.wait_ge(twisted_ready, GROUPS * f + g + 1)
                done = slice(GS * g, GS * g + (GS if f else GS // 2))
                nc.vector.tensor_tensor(dst[:, done], dst[:, done], tln[:, done],
                                        ALU.add).then_inc((x_mid_ready, x_out_ready)[f], 1)

            def ffn_cycles(f):
                dve.wait_ge(consts_ready, 1)
                dve.wait_ge(gf_act, 3 * f + 3)
                nc.vector.tensor_scalar(alpha[:, f:f + 1], gf[:, f, 6:7], range_07, BASE_COUPLING,
                                        ALU.mult, ALU.add).then_inc(alpha_ready, 1)
                dve.wait_ge(alpha_ready, f + 1)
                for s in range(GROUPS, ITEMS):
                    update(f, s)
                finish_part(f, 0)
                finish_coef(f, 0)
                for g in range(GROUPS):
                    finish_straight(f, g)
                    if g + 1 < GROUPS and f:
                        finish_part(f, g + 1)
                        finish_coef(f, g + 1)
                    finish_twisted(f, g)
                    if f == 0:
                        if g + 1 < GROUPS:
                            finish_part(f, g + 1)
                        bn_stats(GROUPS + g)
                        if g + 1 < GROUPS:
                            finish_coef(f, g + 1)
                        bn_moments(GROUPS + g)
                if f == 0:
                    normalise(2 * GROUPS - 1)

            for g in range(2):
                bn_stats(g)
                bn_moments(g)
            for g in range(2, GROUPS):
                normalise(g - 2)
                bn_stats(g)
                bn_moments(g)
            take_pq(0, 0)
            normalise(2)
            normalise(3)
            for g in range(1, GROUPS):
                take_pq(0, g)
            ffn_cycles(0)

            def mix_first(b):
                dve.wait_ge(a_done, b + 1)
                nc.vector.tensor_tensor(am[:, b], bank[6 + b][:, 0:D], A("mask"), ALU.mult).then_inc(am_ready, 1)
                dve.wait_ge(am_ready, b + 1)
                nc.vector.tensor_tensor(ai[:, b], am[:, b], ident, ALU.add)

            def mix_second(b):
                dve.wait_ge(zsum_done, b + 1)
                then(nc.vector.reciprocal(zi[:, b], bank[6 + b][:, D:2 * D]))
                nc.vector.tensor_tensor(mix[:, b], ai[:, b], zi[:, b], ALU.mult).then_inc(mix_ready, 1)

            dve.wait_ge(x_att_loaded, 16 * B)
            dve.wait_ge(p_bias_done, 1)
            for hg in range(GROUPS):
                r = group(x_att, hg).rearrange("p h e -> p (h e)")
                nc.vector.tensor_tensor(r, bank[7][:, :], r, ALU.add).then_inc(p_bias_added, 1)

            dve.wait_ge(att_loaded, 16)
            for n in range(8 + 3):
                if n >= 3:
                    dve.wait_ge(log_done, n - 2)
                    e = qk[:, n - 3].rearrange("p s e -> p (s e)")
                    nc.vector.tensor_tensor(e, e, soft_ps[(n - 3) % 6][:, :], ALU.max).then_inc(soft_done, 1)
                if n < 8:
                    dve.wait_ge(exp_done, n + 1)
                    e = qk[:, n].rearrange("p s e -> p (s e)")
                    nc.vector.tensor_scalar(e, e, EXP_TOP, None, ALU.min).then_inc(clamp_done, 1)
                if n == 7:
                    mix_first(0)
            mix_second(0)
            mix_first(1)
            mix_second(1)
            for g in range(GROUPS):
                dve.wait_ge(mixed_done, g + 1)
                nc.vector.tensor_tensor(og[:, :, GS * g:GS * g + GS, :].rearrange("p h j n -> p j h n"),
                                        bank[2 + g][:, :].rearrange("p (j h n) -> p j h n", j=GS, h=H),
                                        group(gate, g).rearrange("p j (h n) -> p j h n", h=H),
                                        ALU.mult).then_inc(og_ready, 1)
            dve.wait_ge(p_bias_added, GROUPS)
            for hg in range(GROUPS):
                dve.wait_ge(proj_done, hg + 1)
                r = group(x_att, hg).rearrange("p h e -> p (h e)")
                nc.vector.tensor_tensor(r, bank[2 + hg][:, :], r, ALU.add).then_inc(x_att_ready, 1)
                if hg >= 1:
                    bn_moments(2 * GROUPS + hg - 1)
                bn_stats(2 * GROUPS + hg)
                if hg >= 2:
                    normalise(2 * GROUPS + hg - 2)
            bn_moments(3 * GROUPS - 1)
            normalise(3 * GROUPS - 2)
            normalise(3 * GROUPS - 1)
            for g in range(1, GROUPS):
                take_pq(1, g)
            ffn_cycles(1)

        @block.tensor
        def _(pe):
            def keep_warm(free_bank, times):
                for _ in range(times):
                    nc.tensor.matmul(free_bank[:, 0:128], ones_bf[:, :], ones_bf[:, :], start=True, stop=True)

            def transpose_group(use, tiles, first_ready=None):
                if use >= 2:
                    pe.wait_ge(trans_read, use - 1)
                for j, tile in enumerate(tiles):
                    if first_ready is not None:
                        pe.wait_ge(pre_ready, first_ready + j)
                    last = nc.tensor.transpose(trans_ps[use % 2][:, D * j:D * j + D], tile, ident)
                last.then_inc(trans_done, 1)

            def transpose_ln(layer, g, use):
                pe.wait_ge(ln_ready, GROUPS * layer + g + 1)
                if layer:
                    pe.wait_ge(ln_first_ready, GROUPS * (layer - 1) + g + 1)
                transpose_group(use, [ln[:, GS * g + j] for j in range(GS)])

            def products_pq(f, g):
                pe.wait_ge(trans_read, use_ln(f, g) + 1)
                for half in range(2):
                    if f or g:
                        pe.wait_ge(pq_read, 2 * (GROUPS * f + g) + half - 1)
                    for j in range(2):
                        at = D * (GS * g + 2 * half + j)
                        last = nc.tensor.matmul(pq_ps[half][:, 2 * D * j:2 * D * (j + 1)], lnT[:, at:at + D],
                                                early_sb[:, EARLY["w1"][0]:EARLY["w1t"][1]],
                                                start=True, stop=True)
                    last.then_inc(pq_done, 1)

            def transpose_pre(f, s):
                cycle, g = divmod(s, GROUPS)
                if cycle == 0:
                    pe.wait_ge(pq_read, 2 * (GROUPS * f + g) + 2)
                    tiles = [pq[:, GS * g + j, 0] for j in range(GS)]
                    transpose_group(use_pre(f, s), tiles)
                else:
                    tiles = [pre[:, GS * g + j] for j in range(GS)]
                    transpose_group(use_pre(f, s), tiles, first_ready=GS * (2 * GROUPS * f + s - GROUPS) + 1)

            def layer2(f, s):
                n = ITEMS * f + s
                pe.wait_ge(trans_read, use_pre(f, s) + 1)
                if n:
                    pe.wait_ge(gelu2_done, n)
                if n == ITEMS:
                    pe.wait_ge(x_att_ready, 3)
                for half in range(2):
                    last = nc.tensor.matmul(l2_ps[64 * half:64 * half + 64, 0:GW // 2], W("w2"),
                                            h1[:, n % 2, GW // 2 * half:GW // 2 * (half + 1)],
                                            start=True, stop=True)
                last.then_inc(l2_done, 1)

            def layer3(f, s):
                n = ITEMS * f + s
                pe.wait_ge(gelu2_done, n + 1)
                if n:
                    pe.wait_ge(gelu3_done, n)
                if n == ITEMS:
                    pe.wait_ge(x_att_ready, 4)
                for half in range(2):
                    last = nc.tensor.matmul(l3_ps[64 * half:64 * half + 64, 0:D], W("w3"),
                                            h2[:, n % 2, D * half:D * half + D], start=True, stop=True)
                last.then_inc(l3_done, 1)

            def layer4(f, s):
                n = ITEMS * f + s
                pe.wait_ge(gelu3_done, n + 1)
                if n:
                    pe.wait_ge(tanh_done, n)
                nc.tensor.matmul(l4_ps[:, 0:GS], h3[:, n % 2], W("w4"), start=True, stop=True).then_inc(l4_done, 1)

            def context_step(f, k):
                if k == 0:
                    pe.wait_ge(trans_read, use_ln(f, GROUPS - 1) + 1)
                    for g in range(GROUPS):
                        ins = nc.tensor.matmul(gf_ps[0:64, 8:10], W("gc1"), token_sum[:, f, g],
                                               start=(g == 0), stop=(g == GROUPS - 1))
                else:
                    pe.wait_ge(gf_act, 3 * f + k)
                    if k == 1:
                        ins = nc.tensor.matmul(gf_ps[0:32, 16:18], W("gc2", 64), gf[0:64, f, 2:4],
                                               start=True, stop=True)
                    else:
                        ins = nc.tensor.matmul(gf_ps[:, 24:25], g2x[:, f], W("gc3", 32), start=True, stop=True)
                ins.then_inc(gf_pe, 1)

            def ffn(f):
                if f:
                    keep_warm(gf_ps, 25)
                transpose_ln(2 * f, 0, use_ln(f, 0))
                keep_warm(gf_ps, 15)
                products_pq(f, 0)
                transpose_ln(2 * f, 1, use_ln(f, 1))
                keep_warm(gf_ps, 12)
                for k in range(GROUPS):
                    transpose_pre(f, k)
                    if k in (2, 3):
                        context_step(f, 2 * (k - 2))
                    if k >= 2:
                        layer4(f, k - 2)
                    if k + 1 < GROUPS:
                        products_pq(f, k + 1)
                    if k == 2:
                        context_step(f, 1)
                    if k >= 1:
                        layer3(f, k - 1)
                    if k + 2 < GROUPS:
                        transpose_ln(2 * f, k + 2, use_ln(f, k + 2))
                    layer2(f, k)
                transpose_pre(f, GROUPS)
                for k in range(GROUPS, ITEMS + 2):
                    layer4(f, k - 2)
                    if k + 1 < ITEMS:
                        transpose_pre(f, k + 1)
                    if k < ITEMS + 1:
                        layer3(f, k - 1)
                    if k < ITEMS:
                        layer2(f, k)

            def fill(dst, row, stop):
                bias = bias_rows[:, D * ROWS[row]:D * ROWS[row] + D].unsqueeze(1).to_broadcast([128, GS, D])
                return nc.tensor.matmul(dst[:, :].rearrange("p (j e) -> p j e", j=GS), ones_bf[:, :], bias,
                                        start=True, stop=stop, skip_group_check=True)

            def biased(dst, row, tiles, weights):
                fill(dst, row, stop=False)
                for j, tile in enumerate(tiles):
                    last = nc.tensor.matmul(dst[:, D * j:D * j + D], tile, weights, start=False,
                                            stop=(j == GS - 1), skip_group_check=True)
                return last

            def v_and_gate(g, next_group=None):
                if g:
                    pe.wait_ge(proj1_read, 4 * (g - 1) + 3)
                nc.tensor.matmul(bank[4][:, :], A("v"), lnT[:, GW * g:GW * g + GW],
                                 start=True, stop=True).then_inc(proj1_done, 1)
                if next_group is not None:
                    transpose_ln(1, next_group, use_ln_att(next_group))
                if g:
                    pe.wait_ge(proj1_read, 4 * g)
                biased(bank[5], "g", [lnT[:, D * (GS * g + j):D * (GS * g + j + 1)] for j in range(GS)],
                       A("g")).then_inc(proj1_done, 1)

            pe.wait_ge(ones_ready, 1)
            keep_warm(gf_ps, 50)
            pe.wait_ge(early_loaded, 16)
            pe.wait_ge(net_loaded, 16)
            pe.wait_ge(signs_ready, 1)
            ffn(0)
            pe.wait_ge(gelu2_done, ITEMS)
            pe.wait_ge(gelu3_done, ITEMS)
            pe.wait_ge(att_loaded, 16)
            pe.wait_ge(bias_rows_ready, 1)
            keep_warm(gf_ps, 30)
            transpose_ln(1, 0, use_ln_att(0))
            keep_warm(gf_ps, 8)
            fill(bank[7], "p", stop=True).then_inc(p_bias_done, 1)
            for g in range(GROUPS):
                pe.wait_ge(trans_read, use_ln_att(g) + 1)
                for i, name in enumerate(("q1", "k1")):
                    if g:
                        pe.wait_ge(proj1_read, 4 * (g - 1) + i + 1)
                    nc.tensor.matmul(bank[2 + i][:, :], A(name), lnT[:, GW * g:GW * g + GW],
                                     start=True, stop=True).then_inc(proj1_done, 1)
                if g + 1 < GROUPS:
                    v_and_gate(g, g + 1)

            def softplus_inputs(i):
                b, u = divmod(i, 2)
                for x_, (h, row) in enumerate(((h1q, "q2"), (h1k, "k2"))):
                    n = 2 * i + x_
                    if i == 2:
                        pe.wait_ge(trans_read, use_ln_att(GROUPS - 1) + 1)
                    elif i < 2:
                        pe.wait_ge(proj1_read, 4 * (GROUPS - 1) + min(n, 1) + 1)
                    else:
                        pe.wait_ge(soft_done, n - 5)
                    tiles = [h[:, b, 8 * u + 2 * j:8 * u + 2 * j + 2, :].rearrange("p s t -> p (s t)")
                             for j in range(GS)]
                    biased(soft_ps[n % 6], row, tiles, A(row)).then_inc(qk_done, 1)

            def d_sum(b):
                return nc.tensor.matmul(bank[6 + b][:, D:2 * D], A("ones"), A("ones"), start=True, stop=False,
                                        skip_group_check=True)

            def product_qk(i):
                b, u = divmod(i, 2)
                pe.wait_ge(soft_done, 2 * i + 2)
                if i == 0:
                    pe.wait_ge(tanh_done, ITEMS)
                if i == 2:
                    pe.wait_ge(p_bias_added, GROUPS)
                for j in range(GS):
                    nc.tensor.matmul(bank[6 + b][:, 0:D], qk[:, 2 * i + 1, j], qk[:, 2 * i, j],
                                     start=(u == 0 and j == 0), stop=(u == 1 and j == GS - 1))
                if u == 1:
                    d_sum(b).then_inc(a_done, 1)

            def z_sum(b):
                pe.wait_ge(am_ready, b + 1)
                nc.tensor.matmul(bank[6 + b][:, D:2 * D], A("ones"), am[:, b], start=False, stop=True,
                                 skip_group_check=True).then_inc(zsum_done, 1)

            def mix_values(batches, groups):
                pe.wait_ge(mix_ready, batches[-1] + 1)
                for g in groups:
                    for j in range(GS):
                        for b in batches:
                            last = nc.tensor.matmul(bank[2 + g][T * b:T * b + T, D * j:D * j + D],
                                                    vT[:, b, GS * g + j, :], mix[:, b], start=True, stop=True)
                    if b == B - 1:
                        last.then_inc(mixed_done, 1)

            def transpose_og(hg):
                transpose_group(use_og(hg), [og[:, GS * hg + j].rearrange("p j n -> p (j n)") for j in range(GS)])

            softplus_inputs(0)
            softplus_inputs(1)
            softplus_inputs(2)
            product_qk(0)
            softplus_inputs(3)
            product_qk(1)
            pe.wait_ge(soft_done, 4)
            v_and_gate(GROUPS - 1)
            z_sum(0)
            product_qk(2)
            product_qk(3)
            pe.wait_ge(soft_done, 8)
            z_sum(1)
            mix_values([0], [0])
            mix_values([0], [1])
            mix_values([1], [0])
            mix_values([1], [1])
            pe.wait_ge(proj1_read, 4 * GROUPS)
            for g in range(2, GROUPS):
                mix_values([0, 1], [g])
            keep_warm(gf_ps, 15)
            pe.wait_ge(og_ready, GROUPS)
            transpose_og(0)
            for hg in range(GROUPS):
                if hg + 1 < GROUPS:
                    transpose_og(hg + 1)
                pe.wait_ge(trans_read, use_og(hg) + 1)
                for j in range(GS):
                    last = nc.tensor.matmul(bank[2 + hg][:, D * j:D * j + D], ogT[:, GS * hg + j], A("p"),
                                            start=True, stop=True)
                last.then_inc(proj_done, 1)
            pe.wait_ge(x_att_ready, 2)
            ffn(1)


def kernel(**inputs):
    import numpy as np
    import concourse.bacc as bacc
    from concourse import mybir as mb
    from concourse.bass_utils import run_bass_kernel_spmd

    a = {k.replace("L0_", "", 1): np.asarray(v) for k, v in inputs.items()}
    early = np.zeros((128, width(EARLY)), np.float32)
    net = np.zeros((128, width(NET)), np.float32)
    att = np.zeros((128, width(ATT)), np.float32)

    def put(dst, table, name, value, row=0, col=0):
        c = table[name][0] + col
        dst[row:row + value.shape[0], c:c + value.shape[1]] = value

    put(early, EARLY, "ident", np.eye(128, dtype=np.float32))
    w1 = a["ffn_cn_w1"]
    put(early, EARLY, "w1", w1)
    put(early, EARLY, "w1t", np.concatenate([w1[64:96], w1[96:128], w1[0:32], w1[32:64]]))
    columns = dict(b1=(a["ffn_cn_b1"], 1), b2=(a["ffn_cn_b2"], 2), b3=(a["ffn_cn_b3"], 4),
                   q1=(a["attn_q_b1"], 1), k1=(a["attn_k_b1"], 1), v=(a["attn_v_b"], 1), b4=(a["ffn_cn_b4"], 128),
                   gc1=(a["ffn_gc_b1"], 1), gc2=(a["ffn_gc_b2"], 1), gc3=(a["ffn_gc_b3"], 128),
                   range=(a["ffn_adaptive_range"], 128))
    for name, (value, times) in columns.items():
        v = np.tile(value, times)
        early[0:v.shape[0], EARLY["vec"][0] + VEC[name]] = v
    put(net, NET, "w2", a["ffn_cn_w2"])
    for i in range(2):
        put(net, NET, "w3", a["ffn_cn_w3"], 64 * i, 32 * i)
    for i, slot in enumerate((0, 2, 1, 3)):
        put(net, NET, "w4", a["ffn_cn_w4"], 32 * i, slot)
    for i in (1, 2, 3):
        put(net, NET, f"gc{i}", a[f"ffn_gc_w{i}"])
    for name, key in dict(q1="q_w1", k1="k_w1", v="v_w", g="g_w", q2="q_w2", k2="k_w2", p="p_w").items():
        put(att, ATT, name, a["attn_" + key].T)
    put(att, ATT, "mask", np.kron(np.eye(H), np.full((HD, HD), SCALE)).astype(np.float32))
    put(att, ATT, "ones", np.ones((128, 128), np.float32))
    rows = np.tile(np.concatenate([a["attn_g_b"], a["attn_q_b2"], a["attn_k_b2"], a["attn_p_b"]])[None], (3, 1))
    arrays = dict(x=np.ascontiguousarray(a["attn_x"].reshape(B * N, D)), early=early, net=net, att=att,
                  rows=np.ascontiguousarray(rows))

    nc = bacc.Bacc("TRN2", target_bir_lowering=False, num_devices=1)
    args = [nc.dram_tensor(f"in_{k}", v.shape, mb.dt.from_np(v.dtype), kind="ExternalInput").ap()
            for k, v in arrays.items()]
    out = nc.dram_tensor("out_x", (B * N, D), mb.dt.float32, kind="ExternalOutput").ap()
    build(nc, *args, out)
    r = run_bass_kernel_spmd(nc, [{f"in_{k}": v for k, v in arrays.items()}], core_ids=[0])
    return r.results[0]["out_x"].reshape(B, N, D)
```
